# Optimizing a Trainium2 kernel written in Bass

```python
import numpy as np
import jax
import jax.numpy as jnp

def _softmax(x, axis=-1):
    return jax.nn.softmax(x, axis=axis)

def _gelu(x):
    return jax.nn.gelu(x, approximate=True)

def _silu(x):
    return jax.nn.silu(x)

def _sigmoid(x):
    return jax.nn.sigmoid(x)

def _layernorm(x, axis=-1, eps=1e-05):
    m = jnp.mean(x, axis=axis, keepdims=True)
    v = jnp.var(x, axis=axis, keepdims=True)
    return (x - m) / jnp.sqrt(v + eps)

def _scatter_add(tgt, idx, src, axis=0):
    return tgt.at[idx].add(src)

def _segment_sum(src, seg, n):
    return jax.ops.segment_sum(src, seg, n)
kernel_name = 'mk_xattn_ffn_d1_seqx_r8_a53ef8'

def setup_inputs(seed: int=0):
    np.random.seed(seed)
    _w = jnp.asarray

    def _rec_inputs():
        import jax
        import jax.numpy as jnp
        _rk = jax.random.key(seed)
        x = -0.0002928 + 1 * jax.random.normal(jax.random.fold_in(_rk, 1), (16, 256, 128), jnp.float32)
        _lenS = 256 - jax.random.randint(jax.random.fold_in(_rk, 7), (16,), 0, max(1, 256 // 4) + 1, jnp.int32)
        _lenS2 = 64 - jax.random.randint(jax.random.fold_in(_rk, 8), (16,), 0, max(1, 64 // 4) + 1, jnp.int32)
        _ctx_1024P = jax.random.normal(jax.random.fold_in(_rk, 11), (16, 16, 128), jnp.float32)
        _ctx_1024c = jax.random.dirichlet(jax.random.fold_in(_rk, 511), 0.3 * jnp.ones((16,), jnp.float32), (16, 64))
        _ctx_1024t = jnp.einsum('bsk,bkd->bsd', _ctx_1024c, _ctx_1024P)
        _ctx_1024t = _ctx_1024t * jax.lax.rsqrt(jnp.mean(jnp.square(_ctx_1024t)) + 1e-12) * 0.953939
        ctx_1024 = 4.13588e-05 + 0.999923 * (_ctx_1024t + 0.3 * jax.random.normal(jax.random.fold_in(_rk, 611), (16, 64, 128), jnp.float32))
        _validS = jnp.arange(256)[None, :] < _lenS[:, None]
        _validS2 = jnp.arange(64)[None, :] < _lenS2[:, None]
        _causal = jnp.tril(jnp.ones((256, 256), dtype=bool))
        mask_BxS2_ik0 = jnp.where(jnp.broadcast_to(_validS2[:, :], (16, 64)), 0, 1).astype(jnp.int32)
        return (x, ctx_1024, mask_BxS2_ik0)
    x, ctx_1024, mask_BxS2_ik0 = _rec_inputs()

    def _L0_xattn_setup():
        import jax, jax.numpy as jnp
        import numpy as np
        HEADS = 16
        DIM_Q = 128
        DIM_KV = 128
        INNER = 128
        key = jax.random.key(seed)
        k1, k2, k3, k4, k5, k6, k7 = jax.random.split(key, 7)
        B, Lq, Lkv = (2, 256, 512)
        H = jax.random.normal(k1, (B, Lq, DIM_Q), dtype=jnp.float32)
        T = jax.random.normal(k2, (B, Lkv, DIM_KV), dtype=jnp.float32)
        mask = jax.random.randint(k3, (B, Lkv), 0, 2, dtype=jnp.int32)
        s = 0.02
        Wq = jax.random.normal(k4, (DIM_Q, INNER), dtype=jnp.float32) * s
        Wk = jax.random.normal(k5, (DIM_KV, INNER), dtype=jnp.float32) * s
        Wv = jax.random.normal(k6, (DIM_KV, INNER), dtype=jnp.float32) * s
        Wo = jax.random.normal(k7, (INNER, DIM_Q), dtype=jnp.float32) * s
        return {'H': H, 'T': T, 'mask': mask, 'Wq': Wq, 'Wk': Wk, 'Wv': Wv, 'Wo': Wo}
    _L0_xattn_all = _L0_xattn_setup()
    _L0_xattn_in = {k: v for k, v in _L0_xattn_all.items() if k in ('Wq', 'Wk', 'Wv', 'Wo')}
    del _L0_xattn_all

    def _L0_ffn_setup():
        import jax, jax.numpy as jnp
        import numpy as np
        TOP_K = 2
        CAPACITY_FACTOR = 1.25

        def _moe_forward(x, gate_w, wi_gate, wi_up, wo):
            B, S, D = x.shape
            E = wi_gate.shape[0]
            N = B * S
            capacity = max(int(N / E * CAPACITY_FACTOR), 1)
            x_flat = x.reshape(N, D)
            router_logits = x_flat @ gate_w.T
            router_probs = jax.nn.softmax(router_logits, axis=-1)
            top_k_probs, top_k_idx = jax.lax.top_k(router_probs, TOP_K)
            top_k_probs = top_k_probs / jnp.sum(top_k_probs, axis=-1, keepdims=True)
            out = jnp.zeros_like(x_flat)
            experts = jnp.arange(E, dtype=jnp.int32)
            for k in range(TOP_K):
                eid = top_k_idx[:, k]
                ew = top_k_probs[:, k]
                onehot = (eid[:, None] == experts[None, :]).astype(jnp.int32)
                pos_all = jnp.cumsum(onehot, axis=0) - 1
                pos = jnp.take_along_axis(pos_all, eid[:, None].astype(jnp.int32), axis=1)[:, 0]
                valid = pos < capacity
                pos_c = jnp.where(valid, pos, 0)
                disp = jnp.zeros((E, capacity, D), x_flat.dtype).at[eid, pos_c].add(jnp.where(valid[:, None], x_flat, 0.0))
                gate = jax.nn.silu(jnp.einsum('ecd,efd->ecf', disp, wi_gate))
                up = jnp.einsum('ecd,efd->ecf', disp, wi_up)
                expert_out = jnp.einsum('ecf,edf->ecd', gate * up, wo)
                tok_out = expert_out[eid, pos_c]
                out = out + jnp.where(valid[:, None], ew[:, None] * tok_out, 0.0)
            return out.reshape(B, S, D)
        key = jax.random.key(seed)
        k1, k2, k3, k4, k5 = jax.random.split(key, 5)
        B, S, D, F, E = (4, 256, 128, 512, 8)
        return {'x': jax.random.normal(k1, (B, S, D), dtype=jnp.float32), 'gate_w': jax.random.normal(k2, (E, D), dtype=jnp.float32) * 0.02, 'wi_gate': jax.random.normal(k3, (E, F, D), dtype=jnp.float32) * 0.02, 'wi_up': jax.random.normal(k4, (E, F, D), dtype=jnp.float32) * 0.02, 'wo': jax.random.normal(k5, (E, D, F), dtype=jnp.float32) * 0.02}
    _L0_ffn_all = _L0_ffn_setup()
    _L0_ffn_in = {k: v for k, v in _L0_ffn_all.items() if k in ('gate_w', 'wi_gate', 'wi_up', 'wo')}
    del _L0_ffn_all
    return {'x': x, 'ctx_1024': ctx_1024, 'mask_BxS2_ik0': mask_BxS2_ik0, 'L0_xattn_Wq': _L0_xattn_in['Wq'], 'L0_xattn_Wk': _L0_xattn_in['Wk'], 'L0_xattn_Wv': _L0_xattn_in['Wv'], 'L0_xattn_Wo': _L0_xattn_in['Wo'], 'L0_ffn_gate_w': _L0_ffn_in['gate_w'], 'L0_ffn_wi_gate': _L0_ffn_in['wi_gate'], 'L0_ffn_wi_up': _L0_ffn_in['wi_up'], 'L0_ffn_wo': _L0_ffn_in['wo']}

def reference(x, ctx_1024, mask_BxS2_ik0, L0_xattn_Wq, L0_xattn_Wk, L0_xattn_Wv, L0_xattn_Wo, L0_ffn_gate_w, L0_ffn_wi_gate, L0_ffn_wi_up, L0_ffn_wo):
    import jax
    import jax.numpy as jnp

    def _L0_xattn_ref(H, T, mask, Wq, Wk, Wv, Wo):
        import jax, jax.numpy as jnp
        import numpy as np
        HEADS = 16
        DIM_Q = 128
        DIM_KV = 128
        INNER = 128
        B, Lq, _ = H.shape
        Lkv = T.shape[1]
        dph = INNER // HEADS

        def shape(x, L):
            return x.reshape(B, L, HEADS, dph).transpose(0, 2, 1, 3)
        q = shape(H @ Wq, Lq) * dph ** (-0.5)
        k = shape(T @ Wk, Lkv)
        v = shape(T @ Wv, Lkv)
        scores = jnp.einsum('bhqd,bhkd->bhqk', q, k)
        ext = (1.0 - mask.astype(scores.dtype))[:, None, None, :] * jnp.finfo(scores.dtype).min
        scores = scores + ext
        attn = jax.nn.softmax(scores.astype(jnp.float32), axis=-1).astype(scores.dtype)
        out = jnp.einsum('bhqk,bhkd->bhqd', attn, v)
        out = out.transpose(0, 2, 1, 3).reshape(B, Lq, INNER)
        return out @ Wo

    def _L0_ffn_ref(x, gate_w, wi_gate, wi_up, wo):
        import jax, jax.numpy as jnp
        import numpy as np
        TOP_K = 2
        CAPACITY_FACTOR = 1.25

        def _moe_forward(x, gate_w, wi_gate, wi_up, wo):
            B, S, D = x.shape
            E = wi_gate.shape[0]
            N = B * S
            capacity = max(int(N / E * CAPACITY_FACTOR), 1)
            x_flat = x.reshape(N, D)
            router_logits = x_flat @ gate_w.T
            router_probs = jax.nn.softmax(router_logits, axis=-1)
            top_k_probs, top_k_idx = jax.lax.top_k(router_probs, TOP_K)
            top_k_probs = top_k_probs / jnp.sum(top_k_probs, axis=-1, keepdims=True)
            out = jnp.zeros_like(x_flat)
            experts = jnp.arange(E, dtype=jnp.int32)
            for k in range(TOP_K):
                eid = top_k_idx[:, k]
                ew = top_k_probs[:, k]
                onehot = (eid[:, None] == experts[None, :]).astype(jnp.int32)
                pos_all = jnp.cumsum(onehot, axis=0) - 1
                pos = jnp.take_along_axis(pos_all, eid[:, None].astype(jnp.int32), axis=1)[:, 0]
                valid = pos < capacity
                pos_c = jnp.where(valid, pos, 0)
                disp = jnp.zeros((E, capacity, D), x_flat.dtype).at[eid, pos_c].add(jnp.where(valid[:, None], x_flat, 0.0))
                gate = jax.nn.silu(jnp.einsum('ecd,efd->ecf', disp, wi_gate))
                up = jnp.einsum('ecd,efd->ecf', disp, wi_up)
                expert_out = jnp.einsum('ecf,edf->ecd', gate * up, wo)
                tok_out = expert_out[eid, pos_c]
                out = out + jnp.where(valid[:, None], ew[:, None] * tok_out, 0.0)
            return out.reshape(B, S, D)
        return _moe_forward(x, gate_w, wi_gate, wi_up, wo)
    x = x + _L0_xattn_ref(_layernorm(x, axis=-1), ctx_1024, mask_BxS2_ik0, L0_xattn_Wq, L0_xattn_Wk, L0_xattn_Wv, L0_xattn_Wo)
    x = x + _L0_ffn_ref(_layernorm(x, axis=-1), L0_ffn_gate_w, L0_ffn_wi_gate, L0_ffn_wi_up, L0_ffn_wo)
    return x

_drawn_inputs = setup_inputs


def setup_inputs(seed=0):
    import zlib

    import numpy as np

    out = dict(_drawn_inputs(seed))
    spreads = {}
    factors = {'L0_xattn_Wq': 8.0,
     'L0_xattn_Wk': 8.0,
     'L0_ffn_gate_w': 7.776,
     'L0_ffn_wi_gate': 6.801,
     'L0_ffn_wi_up': 6.766,
     'L0_ffn_wo': 6.762}
    for name, (base, spread) in spreads.items():
        noise = np.random.default_rng([zlib.crc32(name.encode()), seed]).standard_normal(out[name].shape)
        drawn = base * np.exp(spread * noise) if base else spread * noise
        out[name] = jnp.asarray(drawn.astype(out[name].dtype))
    for name, factor in factors.items():
        out[name] = (out[name] * factor).astype(out[name].dtype)
    return out
```

```python
from contextlib import ExitStack

import concourse.bass as bass
import numpy as np
from concourse import mybir

F32 = mybir.dt.float32
F32R = mybir.dt.float32r
BF16 = mybir.dt.bfloat16
I32 = mybir.dt.int32
ALU = mybir.AluOpType
ACT = mybir.ActivationFunctionType
AX = mybir.AxisListType

P = 128
B, LQ, LK, D = 16, 256, 64, 128
HEADS, DPH = 16, 8
GROUPS, HG = 4, 4
TOKENS = B * LQ
TILES = TOKENS // P
E, F, TOPK = 8, 512, 2
CAP = int(TOKENS / E * 1.25)
ESLOTS = TOPK * CAP
SLOTS = E * ESLOTS
STILES = ESLOTS // P
ROW = 132
EPS = 1e-5
BIG = float(2.0 ** 127)
SCALE = DPH ** -0.5
ONE_ROW = 96
NROW = ONE_ROW + 1 + HEADS
FT = F // P
CHUNKS = [(0, 4), (4, 4), (8, 2)]

C_IDENT = 0
C_KMASK = C_IDENT + P
C_VMASK = C_KMASK + GROUPS * HG
C_REV = C_VMASK + 2 * P
C_BASE = C_REV + E
C_TRASH = C_BASE + TOPK * E
C_TOKEN = C_TRASH + TILES * TOPK
C_TRI = C_TOKEN + TILES
NCONST = C_TRI + P


def constants():
    c = np.zeros((P, NCONST), np.float32)
    p = np.arange(P)
    c[:, C_IDENT:C_IDENT + P] = np.eye(P)
    km = np.zeros((P, GROUPS, HG), np.float32)
    for r in range(ONE_ROW):
        km[r, :, (r % 32) // DPH] = 1
    km[ONE_ROW] = 1
    for h in range(HEADS):
        km[ONE_ROW + 1 + h, h // HG, h % HG] = 1
    c[:, C_KMASK:C_VMASK] = km.reshape(P, -1)
    vm = np.zeros((P, 2, GROUPS, HG, DPH), np.float32)
    for s in range(2):
        for half in range(2):
            vm[64 * half:64 * half + 64, s, :, 2 * s + half, :] = 1
    c[:, C_VMASK:C_REV] = vm.reshape(P, -1)
    c[:, C_REV:C_BASE] = E - np.arange(E)
    c[:, C_BASE:C_TRASH] = (np.arange(E)[None, :] * ESLOTS + np.arange(TOPK)[:, None] * CAP).reshape(-1)
    token = np.arange(TILES)[None, :] * P + p[:, None]
    c[:, C_TRASH:C_TOKEN] = (SLOTS + token[:, :, None] + TOKENS * np.arange(TOPK)).reshape(P, -1)
    c[:, C_TOKEN:C_TRI] = token
    c[:, C_TRI:] = p[:, None] < p[None, :]
    empty = np.zeros((ESLOTS, ROW), np.float32)
    empty[:, 130] = TOKENS + np.arange(ESLOTS)
    return c, empty, np.zeros((1024, D), np.float32)


def program(nc, x, ctx, mask, wq, wk, wv, wo, gate, wgu, wdn, const, empty, zeros, out):
    slots = nc.dram_tensor("slots", [SLOTS + TOPK * TOKENS, ROW], F32, kind="Internal").ap()
    back = [nc.dram_tensor(f"back{k}", [TOKENS + ESLOTS, D], F32, kind="Internal").ap() for k in range(TOPK)]
    x_t = x.rearrange("(t p) d -> p t d", p=P)
    out_t = out.rearrange("(t p) d -> p t d", p=P)

    with ExitStack() as stack:
        def sb(name, shape, dt=F32, where=stack):
            return where.enter_context(nc.sbuf_tensor(name, shape, dt))

        def sem(name):
            return stack.enter_context(nc.semaphore(name))

        X = sb("X", [P, TILES, D])
        C = sb("C", [P, NCONST])
        W_RAW = [sb(f"w_raw{v}", [P, 2 * F + FT * D]) for v in range(2)]
        W_HI = [sb(f"w_hi{v}", [P, 2 * F], F32R) for v in range(2)]
        W_LO = [sb(f"w_lo{v}", [P, 2 * F], F32R) for v in range(2)]
        XL = [sb(f"xl{v}", [P, STILES, ROW]) for v in range(2)]
        IDX = [sb(f"idx{v}", [P, STILES], I32) for v in range(2)]
        part1 = ExitStack()

        def s1(name, shape, dt=F32):
            return sb(name, shape, dt, part1)

        TRI = s1("tri", [P, P], BF16)
        ONES = s1("ones", [P, P], BF16)
        CTX = s1("ctx", [P, B, 2, LK])
        CTXM = s1("ctxm", [P, B, LK])
        CTX_HI = s1("ctx_hi", [P, B * LK], F32R)
        CTX_LO = s1("ctx_lo", [P, B * LK], F32R)
        MASKI = s1("maski", [P, B, LK], I32)
        MASKF = s1("maskf", [P, B, LK])
        ANY = s1("any", [P, B])
        WQK = s1("wqk", [P, 2, GROUPS, 96])
        WQK_HI = s1("wqk_hi", [P, 2, GROUPS, 96], F32R)
        WQK_LO = s1("wqk_lo", [P, 2, GROUPS, 96], F32R)
        WV = s1("wv", [P, D])
        WO = s1("wo", [P, D])
        GATE = s1("gate", [P, E])
        KC = s1("kc", [P, B, GROUPS, LK])
        VALL = s1("vall", [P, B, D])
        STATS = s1("stats", [P, TILES, 6])
        MV = s1("mv", [P, TILES, 2])
        VE = s1("ve", [P, TILES])
        RSTD = s1("rstd", [P, TILES])
        HALF = s1("half", [P, TILES])
        XN = [s1(f"xn{v}", [P, 2, D]) for v in range(2)]
        XT_HI = [s1(f"xt_hi{v}", [P, LQ], F32R) for v in range(2)]
        XT_LO = [s1(f"xt_lo{v}", [P, LQ], F32R) for v in range(2)]
        QS = [s1(f"qs{v}", [P, GROUPS, LQ], F32R) for v in range(2)]
        KS = [s1(f"ks{v}", [P, GROUPS, HG * LK], F32R) for v in range(2)]
        V2 = [s1(f"v2{v}", [P, 2, GROUPS, 32]) for v in range(2)]
        MNEG = [s1(f"mneg{v}", [P, 2, 1 + HEADS]) for v in range(2)]
        PROBS = [s1(f"probs{v}", [P, GROUPS, 2, LQ]) for v in range(2)]
        RDEN = [s1(f"rden{v}", [P, LQ]) for v in range(2)]
        AT = [s1(f"at{v}", [P, LQ]) for v in range(2)]
        STATS2 = [s1(f"stats2{v}", [P, 2, 6]) for v in range(2)]
        MV2 = [s1(f"mv2{v}", [P, 2, 2]) for v in range(2)]
        VE2 = [s1(f"ve2{v}", [P, 2]) for v in range(2)]
        RSTD2 = [s1(f"rstd2{v}", [P, 2]) for v in range(2)]
        RN = [s1(f"rn{v}", [P, 2, D]) for v in range(2)]
        X2T = [s1(f"x2t{v}", [P, LQ]) for v in range(2)]
        ROWS = s1("rows", [P, 4, ROW])
        LOGIT = s1("logit", [P, 4, E])
        R1 = s1("r1", [P, 4, E])
        R2 = s1("r2", [P, 4, TOPK * E])
        TOP = s1("top", [P, TOPK, 4])
        CODE = s1("code", [P, TOPK, 4])
        OH = s1("oh", [P, 4, TOPK, E], BF16)
        SEEN = s1("seen", [P, TOPK * E], BF16)
        SEENF = s1("seenf", [P, TOPK * E])
        ADDED = s1("added", [P, TOPK * E])
        DELTA = s1("delta", [P, 4])
        EXPD = s1("expd", [P, 4])
        DEN = s1("den", [P, 4])
        RK = s1("rk", [P, 4, TOPK])
        SB = s1("sb", [P, 4, TOPK])
        OKAY = s1("okay", [P, 4, TOPK])
        SLOTF = s1("slotf", [P, 4, TOPK])
        SLOT = s1("slot", [P, 4 * TOPK], I32)
        part1.close()
        part2 = ExitStack()

        def s2(name, shape, dt=F32):
            return sb(name, shape, dt, part2)

        EX_HI = [s2(f"ex_hi{v}", [P, ESLOTS], F32R) for v in range(2)]
        EX_LO = [s2(f"ex_lo{v}", [P, ESLOTS], F32R) for v in range(2)]
        SG = [s2(f"sg{v}", [P, 512]) for v in range(2)]
        H = [s2(f"h{v}", [P, FT, 512]) for v in range(2)]
        YS = [s2(f"ys{v}", [P, 4, D]) for v in range(2)]
        part2.close()
        part3 = ExitStack()
        FB = [[sb(f"fb{k}{q}", [P, 8, D], F32, part3) for q in range(4)] for k in range(TOPK)]
        part3.close()

        BANK = [stack.enter_context(nc.psum_tensor(f"bank{i}", [P, 512], F32)) for i in range(8)]
        MX, ST, QP, OD, M0, M1 = BANK[0:2], BANK[2:4], BANK[4], BANK[5], BANK[6], BANK[7]
        GATE_PS, UP_PS, TB, Y_PS = BANK[0:2], BANK[2:4], BANK[4:6], BANK[6:8]

        const_in, x_in, mask_in, ctx_in, w_in = sem("const_in"), sem("x_in"), sem("mask_in"), sem("ctx_in"), sem("w_in")
        ext_in = sem("ext_in")
        filled = sem("filled")
        raw_in = [sem(f"raw_in{v}") for v in range(2)]
        setup = sem("setup")
        wsplit = sem("wsplit")
        ctx_split = sem("ctx_split")
        pool_setup = sem("pool_setup")
        k_full, k_hi, k_used = sem("k_full"), sem("k_hi"), sem("k_used")
        v_full, v_used = sem("v_full"), sem("v_used")
        ve_ready, rstd_ready = sem("ve_ready"), sem("rstd_ready")
        xn_ready, tx_full, xth_ready, xtl_ready = sem("xn_ready"), sem("tx_full"), sem("xth_ready"), sem("xtl_ready")
        qp_full, qhi_ready, qs_ready = sem("qp_full"), sem("qhi_ready"), sem("qs_ready")
        ks_ready, v2_ready = sem("ks_ready"), sem("v2_ready")
        mx_full, m_ready, mt_full, aug_ready = sem("mx_full"), sem("m_ready"), sem("mt_full"), sem("aug_ready")
        st_full, p_ready, pv_full = sem("st_full"), sem("p_ready"), sem("pv_full")
        rden_ready, at_ready, wo_full, x1_ready = sem("rden_ready"), sem("at_ready"), sem("wo_full"), sem("x1_ready")
        ln2_step, ve2_ready, rstd2_ready, rn_ready = sem("ln2_step"), sem("ve2_ready"), sem("rstd2_ready"), sem("rn_ready")
        tx2_full, x2t_ready, lg_full, logit_ready = sem("tx2_full"), sem("x2t_ready"), sem("lg_full"), sem("logit_ready")
        route_step = sem("route_step")
        oh_ready, rk_full, delta_ready, expd_ready = sem("oh_ready"), sem("rk_full"), sem("delta_ready"), sem("expd_ready")
        routed, rows_ready, sent = sem("routed"), sem("rows_ready"), sem("sent")
        xl_in = [sem(f"xl_in{v}") for v in range(2)]
        w_hi_ready, w_ready = sem("w_hi_ready"), sem("w_ready")
        tb_full, ex_hi_ready, ex_ready, idx_ready = sem("tb_full"), sem("ex_hi_ready"), sem("ex_ready"), sem("idx_ready")
        gu_full, sg_ready, h_ready, dn_full, y_ready = sem("gu_full"), sem("sg_ready"), sem("h_ready"), sem("dn_full"), sem("y_ready")
        returned = [sem(f"returned{v}") for v in range(2)]
        fb_in = [sem(f"fb_in{q}") for q in range(4)]
        add_step, out_ready, stored = sem("add_step"), sem("out_ready"), sem("stored")

        IDENT = C[:, C_IDENT:C_IDENT + P]
        KMASK = C[:, C_KMASK:C_VMASK]
        VMASK = C[:, C_VMASK:C_REV].rearrange("p (s g c) -> p s g c", s=2, g=GROUPS)

        def over_batches(eng, step, first=-1, last=17):
            for i in range(first, 4):
                step(0, i)
            with eng.Fori(2, 7) as it:
                step(it, 0)
                step(it, 1)
            for i in range(14, last + 1):
                step(0, i)

        def present(it, off):
            if not isinstance(it, int):
                return True, True, True, True
            return off + 1 < B, 0 <= off < B, 1 <= off <= B, 2 <= off <= B + 1

        def wait(eng, s, value):
            if not isinstance(value, int) or value > 0:
                eng.wait_ge(s, value)

        def held(eng, value):
            return value if isinstance(value, int) else eng.to_reg(value)

        def over_experts(eng, pair):
            pair(0, False)
            with eng.Fori(1, E // 2 - 1) as it:
                pair(it, False)
            pair(E // 2 - 1, True)

        RETURNS = [[0, 0], [4, 0], [4, 4], [6, 4], [6, 8], [10, 8], [10, 10]]

        block = stack.enter_context(nc.Block())

        @block.sync
        def _(sp):
            sp.dma_start(C[:], const).then_inc(const_in, 16)
            sp.dma_start(MASKI[:].rearrange("p b k -> p (b k)"),
                         mask.rearrange("b k -> (b k)").rearrange("(a n) -> a n", a=1).to_broadcast([P, B * LK])
                         ).then_inc(mask_in, 16)
            sp.dma_start(CTX[:], ctx).then_inc(ctx_in, 16)
            sp.dma_start(WQK[:, 0], wq).then_inc(w_in, 16)
            sp.dma_start(WQK[:, 1], wk).then_inc(w_in, 16)
            sp.dma_start(WV[:], wv).then_inc(w_in, 16)
            sp.dma_start(WO[:], wo).then_inc(w_in, 16)
            sp.dma_start(GATE[:], gate).then_inc(w_in, 16)
            sp.wait_ge(setup, 5)
            sp.wait_ge(pool_setup, 1)
            for g in range(GROUPS):
                sp.dma_start(KC[ONE_ROW:ONE_ROW + 1, :, g, :], MASKF[ONE_ROW:ONE_ROW + 1]).then_inc(ext_in, 16)
            for e in range(E):
                sp.dma_start(slots[e * ESLOTS:(e + 1) * ESLOTS, :], empty).then_inc(filled, 16)
            for k in range(TOPK):
                for q in range(TOKENS // 1024):
                    sp.dma_start(back[k][q * 1024:(q + 1) * 1024, :], zeros).then_inc(filled, 16)
            for v in range(2):
                sp.dma_start(W_RAW[v][:, 0:2 * F], wgu[v]).then_inc(raw_in[v], 16)
                sp.dma_start(W_RAW[v][:, 2 * F:], wdn[v]).then_inc(raw_in[v], 16)
            sp.wait_ge(sent, 16 * 8 * (B // 2))
            for v in range(2):
                sp.dma_start(XL[v][:], slots[v * ESLOTS:(v + 1) * ESLOTS, :].rearrange("(t p) c -> p t c", p=P)
                             ).then_inc(xl_in[v], 16)

            def pair(it, last):
                for v in range(2):
                    if last:
                        continue
                    sp.wait_ge(y_ready, 6 * it + 3 * v + 3)
                    e = 2 * it + (v + 2)
                    sp.dma_start(W_RAW[v][:, 0:2 * F], wgu[bass.ds(e, 1)].rearrange("a p f -> (a p) f")).then_inc(raw_in[v], 16)
                    sp.dma_start(W_RAW[v][:, 2 * F:], wdn[bass.ds(e, 1)].rearrange("a p f -> (a p) f")).then_inc(raw_in[v], 16)
                    sp.dma_start(XL[v][:], slots[bass.ds(e * ESLOTS, ESLOTS), :].rearrange("(t p) c -> p t c", p=P)
                                 ).then_inc(xl_in[v], 16)

            over_experts(sp, pair)
            for v in range(2):
                sp.wait_ge(returned[v], 16 * 10 * (E // 2))
            for q in range(4):
                for k in range(TOPK):
                    sp.dma_start(FB[k][q][:], back[k][q * 1024:(q + 1) * 1024, :].rearrange("(t p) d -> p t d", p=P)
                                 ).then_inc(fb_in[q], 16)
            for q in range(4):
                sp.wait_ge(out_ready, q + 1)
                sp.dma_start(out_t[:, 8 * q:8 * q + 8, :], X[:, 8 * q:8 * q + 8, :]).then_inc(stored, 16)
            sp.wait_ge(stored, 64)

        @block.gpsimd
        def _(pool):
            nc.gpsimd.memset(KC[ONE_ROW:, :, :, :], 1.0).then_inc(pool_setup, 1)
            pool.wait_ge(pool_setup, 1)
            nc.gpsimd.memset(HALF[:], -0.5).then_inc(pool_setup, 1)
            pool.wait_ge(pool_setup, 2)
            pool.wait_ge(ve_ready, 1)
            nc.gpsimd.tensor_tensor(RSTD[:], VE[:], HALF[:], ALU.pow).then_inc(rstd_ready, 1)
            pool.wait_ge(const_in, 16)
            pool.wait_ge(k_used, 8)
            pool.wait_ge(ext_in, 64)
            pool.wait_ge(v_used, 4)

            def spread_keys(it, off, c):
                i = 2 * it + (off + c)
                v = (off + c) % 2
                wait(pool, st_full, 4 * i - 4)
                nc.gpsimd.tensor_tensor(
                    KS[v][0:NROW].rearrange("p g (h k) -> p g h k", h=HG),
                    KC[0:NROW, bass.ds(i, 1)].rearrange("p a g k -> p (a g) k").unsqueeze(2).to_broadcast([NROW, GROUPS, HG, LK]),
                    KMASK[0:NROW].rearrange("p (g h) -> p g h", g=GROUPS).unsqueeze(3).to_broadcast([NROW, GROUPS, HG, LK]),
                    ALU.mult).then_inc(ks_ready, 1)

            def spread_values(it, off):
                i = 2 * it + off
                wait(pool, pv_full, i - 1)
                nc.gpsimd.tensor_tensor(
                    V2[off % 2][:].rearrange("p s g c -> p s (g c)"),
                    VALL[:, bass.ds(i, 1), :].to_broadcast([P, 2, D]),
                    VMASK.rearrange("p s g c -> p s (g c)"), ALU.mult).then_inc(v2_ready, 1)

            def send(r, tiles):
                for t in tiles:
                    for k in range(TOPK):
                        nc.gpsimd.indirect_dma_start(
                            out=slots[:, :], out_offset=bass.IndirectOffsetOnAxis(ap=SLOT[:, 2 * t + k:2 * t + k + 1], axis=0),
                            in_=ROWS[:, t, :], in_offset=None).then_inc(sent, 16)

            def step(it, off):
                nxt, cur, prev, prev2 = present(it, off)
                u = off % 2
                if nxt:
                    spread_keys(it, off, 1)
                if cur:
                    spread_values(it, off)
                r = it + (off - 4) // 2
                if u == 0 and (not isinstance(it, int) or off >= 4):
                    pairs = held(pool, r + 1)
                    pool.wait_ge(filled, 16 * (E + TOPK * TOKENS // 1024))
                    pool.wait_ge(routed, pairs)
                    pool.wait_ge(rows_ready, pairs)
                    send(r, range(4))
                if off % 2 == 1 and prev2:
                    h = it + (off - 3) // 2
                    left, normed = held(pool, 128 * h), held(pool, 2 * h + 2)
                    pool.wait_ge(setup, 7)
                    wait(pool, sent, left)
                    wait(pool, rn_ready, normed)
                    for v in range(2):
                        ins = nc.gpsimd.tensor_copy(ROWS[:, 2 * v:2 * v + 2, 0:D], RN[v][:])
                    ins.then_inc(rows_ready, 1)
                if prev:
                    i = 2 * it + off
                    wait(pool, ve2_ready, i)
                    nc.gpsimd.tensor_tensor(RSTD2[(off - 1) % 2][:], VE2[(off - 1) % 2][:], HALF[:, 0:2], ALU.pow
                                            ).then_inc(rstd2_ready, 1)

            over_batches(pool, step)

            def split_weights(e, v, loads):
                loaded, used = held(pool, 32 * loads), held(pool, 12 * e - 12)
                pool.wait_ge(const_in, 16)
                pool.wait_ge(raw_in[v], loaded)
                wait(pool, gu_full, used)
                nc.gpsimd.tensor_copy(W_HI[v][:], W_RAW[v][:, 0:2 * F]).then_inc(w_hi_ready, 1)
                pool.wait_ge(w_hi_ready, e + 1)
                nc.gpsimd.tensor_tensor(W_LO[v][:], W_RAW[v][:, 0:2 * F], W_HI[v][:].bitcast(F32), ALU.subtract
                                        ).then_inc(w_ready, 1)

            split_weights(0, 0, 1)
            pool.wait_ge(routed, B // 2)
            pool.wait_ge(rows_ready, B // 2)
            send(B // 2 - 1, range(4))

            def pair(it, last):
                for v in range(2):
                    if not (last and v == 1):
                        split_weights(2 * it + (v + 1), 1 - v, it + (v + 1))
                    for c, (t0, nt) in enumerate(CHUNKS):
                        n = 3 * v + c
                        rows = held(pool, 6 * it + (n + 1))
                        pool.wait_ge(filled, 16 * (E + TOPK * TOKENS // 1024))
                        pool.wait_ge(y_ready, rows)
                        for t in range(nt):
                            j = t0 + t
                            nc.gpsimd.indirect_dma_start(
                                out=back[j * P // CAP][:, :],
                                out_offset=bass.IndirectOffsetOnAxis(ap=IDX[v][:, j:j + 1], axis=0),
                                in_=YS[n % 2][:, t, :], in_offset=None).then_inc(returned[n % 2], 16)

            over_experts(pool, pair)
            for v in range(2):
                pool.wait_ge(returned[v], 16 * 10 * (E // 2))

        @block.scalar
        def _(act):
            for q in range(4):
                act.dma_start(X[:, 8 * q:8 * q + 8, :], x_t[:, 8 * q:8 * q + 8, :]).then_inc(x_in, 16)
            act.wait_ge(w_in, 80)
            nc.scalar.copy(WQK_HI[:], WQK[:]).then_inc(wsplit, 1)
            act.wait_ge(setup, 3)
            nc.scalar.copy(CTX_HI[:], CTXM[:].rearrange("p b k -> p (b k)")).then_inc(ctx_split, 1)
            for n in range(8):
                g, half = n // 2, n % 2
                act.wait_ge(k_full, n + 1)
                nc.scalar.copy(KC[0:96, 8 * half:8 * half + 8, g, :].bitcast(F32R),
                               MX[n % 2][0:96, :].rearrange("p (b k) -> p b k", k=LK)).then_inc(k_hi, 1)
            for n in range(4):
                act.wait_ge(v_full, n + 1)
                nc.scalar.copy(VALL[:, 4 * n:4 * n + 4, :], ST[n % 2][:].rearrange("p (b d) -> p b d", d=D)).then_inc(v_used, 1)

            def exps(it, off, c, j):
                i = 2 * it + (off + c)
                act.wait_ge(st_full, 4 * i + (j + 1))
                if j == 0:
                    wait(act, pv_full, i - 1)
                nc.scalar.activation(PROBS[(off + c) % 2][:, j].rearrange("p s q -> p (s q)"), ST[j % 2][:], ACT.Exp
                                     ).then_inc(p_ready, 1)

            def step(it, off):
                nxt, cur, prev, prev2 = present(it, off)
                i = 2 * it + off
                u = off % 2
                if prev:
                    exps(it, off, -1, 2)
                if nxt:
                    act.wait_ge(tx_full, i + 2)
                    wait(act, qp_full, 2 * i)
                    nc.scalar.copy(XT_HI[1 - u][:], M0[:, 0:LQ]).then_inc(xth_ready, 1)
                if prev2:
                    act.wait_ge(tx2_full, i - 1)
                    wait(act, lg_full, i - 3)
                    nc.scalar.copy(X2T[u][:], M1[:, 0:LQ]).then_inc(x2t_ready, 1)
                if prev:
                    exps(it, off, -1, 3)
                if nxt:
                    for h in range(2):
                        act.wait_ge(qp_full, 2 * i + (3 + h))
                        if h == 0:
                            wait(act, st_full, 4 * i)
                        nc.scalar.mul(QS[1 - u][0:96, 2 * h:2 * h + 2, :].rearrange("p g q -> p (g q)"), QP[0:96, :], SCALE
                                      ).then_inc(qhi_ready, 1)
                if cur:
                    act.wait_ge(mt_full, i + 1)
                    nc.scalar.copy(QS[u][ONE_ROW:NROW, :, :],
                                   M0[0:1 + HEADS, 0:LQ].unsqueeze(1).to_broadcast([1 + HEADS, GROUPS, LQ])).then_inc(aug_ready, 1)
                    exps(it, off, 0, 0)
                    exps(it, off, 0, 1)
                if u == 1 and prev2:
                    r = it + (off - 3) // 2
                    act.wait_ge(delta_ready, r + 1)
                    nc.scalar.activation(EXPD[:], DELTA[:], ACT.Exp).then_inc(expd_ready, 1)

            over_batches(act, step)

            def slots_hi(tn, v):
                for c, (t0, nt) in enumerate(CHUNKS):
                    act.wait_ge(tb_full, tn + (c + 1))
                    nc.scalar.copy(EX_HI[v][:, t0 * P:(t0 + nt) * P], TB[(3 * v + c) % 2][:, 0:nt * P]).then_inc(ex_hi_ready, 1)

            slots_hi(0, 0)

            def pair(it, last):
                for v in range(2):
                    for c, (t0, nt) in enumerate(CHUNKS):
                        for f in range(FT):
                            m = 12 * v + 4 * c + f
                            act.wait_ge(gu_full, 24 * it + (m + 1))
                            wait(act, h_ready, 24 * it + (m - 1))
                            nc.scalar.activation(SG[m % 2][:, 0:nt * P], GATE_PS[m % 2][:, 0:nt * P], ACT.Silu).then_inc(sg_ready, 1)
                    if not (last and v == 1):
                        slots_hi(6 * it + (3 * v + 3), 1 - v)

            over_experts(act, pair)

        @block.tensor
        def _(pe):
            def product3(ps, hi, lo, m_hi, m_lo):
                nc.tensor.matmul(ps, hi, m_hi, start=True, stop=False)
                nc.tensor.matmul(ps, lo, m_hi, start=False, stop=False)
                return nc.tensor.matmul(ps, hi, m_lo, start=False, stop=True)

            pe.wait_ge(setup, 7)
            pe.wait_ge(wsplit, 2)
            pe.wait_ge(ctx_split, 2)
            for n in range(8):
                g, half = n // 2, n % 2
                if n >= 2:
                    pe.wait_ge(k_used, n - 1)
                cols = slice(512 * half, 512 * half + 512)
                product3(MX[n % 2][0:96, :], WQK_HI[:, 1, g, :], WQK_LO[:, 1, g, :], CTX_HI[:, cols], CTX_LO[:, cols]
                         ).then_inc(k_full, 1)
            for n in range(4):
                if n >= 2:
                    pe.wait_ge(v_used, n - 1)
                for b in range(4):
                    mm = nc.tensor.matmul(ST[n % 2][:, b * D:(b + 1) * D], CTX[:, 4 * n + b].rearrange("p a k -> p (a k)"), WV[:],
                                          start=True, stop=True)
                mm.then_inc(v_full, 1)
            pe.wait_ge(k_used, 8)
            pe.wait_ge(v_used, 4)

            def row_scores(it, off, t):
                i, u = 2 * it + off, off % 2
                if t == 0:
                    pe.wait_ge(qs_ready, 2 * i + 2)
                    pe.wait_ge(ks_ready, i + 1)
                wait(pe, m_ready, 2 * i + t)
                for g in range(GROUPS):
                    mm = nc.tensor.matmul(MX[g // 2][:, (g % 2) * 256:(g % 2) * 256 + 256],
                                          QS[u][0:ONE_ROW + 1, g, t * P:(t + 1) * P], KS[u][0:ONE_ROW + 1, g, :],
                                          start=True, stop=True)
                mm.then_inc(mx_full, 1)

            def scores(it, off, c, j):
                i, u = 2 * it + (off + c), (off + c) % 2
                if j == 0:
                    pe.wait_ge(aug_ready, i + 1)
                wait(pe, p_ready, 4 * i + (j - 1))
                for s in range(2):
                    mm = nc.tensor.matmul(ST[j % 2][:, s * LQ:(s + 1) * LQ], KS[u][0:NROW, j, s * P:(s + 1) * P],
                                          QS[u][0:NROW, j, :], start=True, stop=True)
                mm.then_inc(st_full, 1)

            def queries(it, off, h):
                i, v = 2 * it + off, (off + 1) % 2
                if h == 0:
                    pe.wait_ge(xtl_ready, i + 2)
                wait(pe, qs_ready, 2 * i + (2 + h))
                for gg in range(2):
                    g = 2 * h + gg
                    mm = product3(QP[0:96, gg * LQ:(gg + 1) * LQ], WQK_HI[:, 0, g, :], WQK_LO[:, 0, g, :], XT_HI[v][:], XT_LO[v][:])
                mm.then_inc(qp_full, 1)

            def step(it, off):
                nxt, cur, prev, prev2 = present(it, off)
                i, u = 2 * it + off, off % 2
                if cur:
                    row_scores(it, off, 0)
                if prev:
                    scores(it, off, -1, 2)
                if nxt:
                    pe.wait_ge(xn_ready, i + 2)
                    wait(pe, aug_ready, i)
                    for t in range(2):
                        mm = nc.tensor.transpose(M0[:, t * P:(t + 1) * P], XN[1 - u][:, t, :], IDENT)
                    mm.then_inc(tx_full, 1)
                if prev2:
                    pe.wait_ge(rn_ready, i - 1)
                    if u == 0:
                        wait(pe, routed, it + (off - 2) // 2)
                    for t in range(2):
                        mm = nc.tensor.transpose(M1[:, t * P:(t + 1) * P], RN[u][:, t, :], IDENT)
                    mm.then_inc(tx2_full, 1)
                if prev:
                    scores(it, off, -1, 3)
                if cur:
                    row_scores(it, off, 1)
                if prev2:
                    pe.wait_ge(x2t_ready, i - 1)
                    for t in range(2):
                        mm = nc.tensor.matmul(M1[:, t * E:(t + 1) * E], X2T[u][:, t * P:(t + 1) * P], GATE[:], start=True, stop=True)
                    mm.then_inc(lg_full, 1)
                if nxt:
                    queries(it, off, 0)
                if prev:
                    pe.wait_ge(p_ready, 4 * i)
                    pe.wait_ge(v2_ready, i)
                    wait(pe, at_ready, i - 1)
                    for what in range(2):
                        for s in range(2):
                            for g in range(GROUPS):
                                w = V2[1 - u][:, s, g, :] if what == 0 else VMASK[:, s, g, :]
                                mm = nc.tensor.matmul(OD[32 * g:32 * g + 32, what * LQ:(what + 1) * LQ], w,
                                                      PROBS[1 - u][:, g, s, :], start=(s == 0), stop=(s == 1))
                    mm.then_inc(pv_full, 1)
                if nxt:
                    queries(it, off, 1)
                if cur:
                    pe.wait_ge(m_ready, 2 * i + 2)
                    if nxt:
                        pe.wait_ge(xtl_ready, i + 2)
                    else:
                        pe.wait_ge(aug_ready, i)
                    for t in range(2):
                        mm = nc.tensor.transpose(M0[0:1 + HEADS, t * P:(t + 1) * P], MNEG[u][:, t, :], IDENT)
                    mm.then_inc(mt_full, 1)
                if prev:
                    pe.wait_ge(at_ready, i)
                    if prev2:
                        pe.wait_ge(logit_ready, i - 1)
                    for t in range(2):
                        mm = nc.tensor.matmul(M1[:, t * D:(t + 1) * D], AT[1 - u][:, t * P:(t + 1) * P], WO[:], start=True, stop=True)
                    mm.then_inc(wo_full, 1)
                if cur:
                    scores(it, off, 0, 0)
                    scores(it, off, 0, 1)
                if u == 1 and prev2:
                    r = it + (off - 3) // 2
                    pe.wait_ge(oh_ready, r + 1)
                    if prev:
                        pe.wait_ge(x1_ready, i)
                    n = TOPK * E
                    ranks = M1[:, 0:4 * n]
                    oh = OH[:].rearrange("p t k e -> p t (k e)")
                    nc.tensor.matmul(ranks, TRI[:], oh.rearrange("p t n -> p (t n)"), start=True, stop=False, skip_group_check=True)
                    for t in range(3):
                        nc.tensor.matmul(ranks[:, (t + 1) * n:], ONES[:], oh[:, t:t + 1, :].to_broadcast([P, 3 - t, n]),
                                         start=False, stop=False, skip_group_check=True)
                    nc.tensor.matmul(ranks, ONES[:], SEEN[:].unsqueeze(1).to_broadcast([P, 4, n]),
                                     start=False, stop=True, skip_group_check=True).then_inc(rk_full, 1)

            over_batches(pe, step)

            def turn_slots(tn, loads, v):
                pe.wait_ge(xl_in[v], 16 * loads)
                for c, (t0, nt) in enumerate(CHUNKS):
                    wait(pe, ex_ready, tn + (c - 1))
                    for t in range(nt):
                        mm = nc.tensor.transpose(TB[(3 * v + c) % 2][:, t * P:(t + 1) * P], XL[v][:, t0 + t, 0:D], IDENT)
                    mm.then_inc(tb_full, 1)

            def down(it, n, v, nt):
                pe.wait_ge(h_ready, 24 * it + 4 * (n + 1))
                if n >= 2 or not isinstance(it, int):
                    wait(pe, y_ready, 6 * it + (n - 1))
                for t in range(nt):
                    for f in range(FT):
                        mm = nc.tensor.matmul(Y_PS[n % 2][:, t * D:(t + 1) * D], H[n % 2][:, f, t * P:(t + 1) * P],
                                              W_RAW[v][:, 2 * F + f * D:2 * F + (f + 1) * D], start=(f == 0), stop=(f == FT - 1))
                mm.then_inc(dn_full, 1)

            turn_slots(0, 1, 0)

            def pair(it, last):
                for v in range(2):
                    pe.wait_ge(w_ready, 2 * it + (v + 1))
                    for c, (t0, nt) in enumerate(CHUNKS):
                        n = 3 * v + c
                        pe.wait_ge(ex_ready, 6 * it + (n + 1))
                        cols = slice(t0 * P, (t0 + nt) * P)
                        for f in range(FT):
                            m = 4 * n + f
                            wait(pe, h_ready, 24 * it + (m - 1))
                            for ps, w0 in ((GATE_PS, 0), (UP_PS, F)):
                                w = slice(w0 + f * P, w0 + (f + 1) * P)
                                mm = product3(ps[m % 2][:, 0:nt * P], W_HI[v][:, w], W_LO[v][:, w], EX_HI[v][:, cols], EX_LO[v][:, cols])
                            mm.then_inc(gu_full, 1)
                            if f == 1 and c > 0:
                                down(it, n - 1, v, CHUNKS[c - 1][1])
                    if not (last and v == 1):
                        turn_slots(6 * it + (3 * v + 3), it + (v + 1), 1 - v)
                    down(it, 3 * v + 2, v, CHUNKS[2][1])

            over_experts(pe, pair)

        @block.vector
        def _(dve):
            dve.wait_ge(mask_in, 16)
            nc.vector.tensor_copy(MASKF[:], MASKI[:]).then_inc(setup, 1)
            dve.wait_ge(setup, 1)
            nc.vector.tensor_reduce(ANY[:], MASKF[:], AX.X, ALU.max).then_inc(setup, 1)
            dve.wait_ge(setup, 2)
            dve.wait_ge(ctx_in, 16)
            any_b = ANY[:].unsqueeze(2).to_broadcast([P, B, LK])
            nc.vector.tensor_tensor(CTXM[:], CTX[:, :, 0, :], any_b, ALU.mult).then_inc(setup, 1)
            nc.vector.tensor_scalar(MASKF[:], MASKF[:], -1.0, BIG, ALU.add, ALU.mult).then_inc(setup, 1)
            dve.wait_ge(setup, 4)
            nc.vector.tensor_tensor(MASKF[:], MASKF[:], any_b, ALU.mult).then_inc(setup, 1)
            dve.wait_ge(wsplit, 1)
            nc.vector.tensor_tensor(WQK_LO[:], WQK[:], WQK_HI[:].bitcast(F32), ALU.subtract).then_inc(wsplit, 1)
            dve.wait_ge(ctx_split, 1)
            nc.vector.tensor_tensor(CTX_LO[:], CTXM[:].rearrange("p b k -> p (b k)"), CTX_HI[:].bitcast(F32), ALU.subtract
                                    ).then_inc(ctx_split, 1)
            dve.wait_ge(const_in, 16)
            nc.vector.tensor_copy(TRI[:], C[:, C_TRI:C_TRI + P]).then_inc(setup, 1)
            nc.vector.memset(ONES[:], 1.0)
            nc.vector.memset(SEEN[:], 0.0)
            nc.vector.memset(SEENF[:], 0.0)
            nc.vector.memset(ROWS[:, :, D:ROW], 0.0)
            for v in range(2):
                nc.vector.memset(MNEG[v][:], 1.0)
                nc.vector.memset(QS[v][ONE_ROW:ONE_ROW + 1, :, :].bitcast(F32), 1.0)
            nc.vector.memset(EXPD[:], 0.0).then_inc(setup, 1)
            for n in range(8):
                g, half = n // 2, n % 2
                dve.wait_ge(k_hi, n + 1)
                lo = KC[64:96, 8 * half:8 * half + 8, g, :]
                nc.vector.tensor_tensor(lo, MX[n % 2][64:96, :].rearrange("p (b k) -> p b k", k=LK), lo, ALU.subtract).then_inc(k_used, 1)
            dve.wait_ge(x_in, 64)
            for t in range(TILES):
                ins = nc.vector.bn_stats(STATS[:, t, :], X[:, t, :])
            ins.then_inc(setup, 1)
            dve.wait_ge(setup, 8)
            for t in range(TILES):
                ins = nc.vector.bn_aggr(MV[:, t, :], STATS[:, t, :])
            ins.then_inc(setup, 1)
            dve.wait_ge(setup, 9)
            nc.vector.tensor_scalar(VE[:], MV[:, :, 1], EPS, None, ALU.add).then_inc(ve_ready, 1)
            dve.wait_ge(rstd_ready, 1)

            def norm(i, v):
                wait(dve, tx_full, i - 1)
                for t in range(2):
                    tile = 2 * i + t
                    ins = nc.vector.tensor_scalar(
                        XN[v][:, t, :], X[:, bass.ds(tile, 1), :].rearrange("p a d -> p (a d)"),
                        MV[:, bass.ds(tile, 1), 0], RSTD[:, bass.ds(tile, 1)], ALU.subtract, ALU.mult)
                ins.then_inc(xn_ready, 1)

            norm(0, 0)
            norm(1, 1)

            ROUTE = 19

            def row_max(it, off, t):
                i, u = 2 * it + off, off % 2
                dve.wait_ge(mx_full, 2 * i + (t + 1))
                if t == 0:
                    wait(dve, mt_full, i - 1)
                for b in range(2):
                    ins = nc.vector.tensor_reduce(MNEG[u][:, t, 1 + 8 * b:9 + 8 * b], MX[b][:].rearrange("p (h k) -> p h k", k=LK),
                                                  AX.X, ALU.max, negate=True)
                ins.then_inc(m_ready, 1)

            def queries_lo(it, off, h):
                i, v = 2 * it + off, (off + 1) % 2
                dve.wait_ge(qhi_ready, 2 * i + (3 + h))
                mid = QS[v][32:64, 2 * h:2 * h + 2, :].rearrange("p g q -> p (g q)")
                nc.vector.scalar_tensor_tensor(out=mid, in0=QP[32:64, :], scalar=SCALE, in1=mid.bitcast(F32),
                                               op0=ALU.mult, op1=ALU.subtract).then_inc(qs_ready, 1)

            def choose(r):
                n = [0]

                def link(ins):
                    n[0] += 1
                    ins.then_inc(route_step, 1)
                    dve.wait_ge(route_step, ROUTE * r + n[0])

                rev = C[:, C_REV:C_BASE].unsqueeze(1).to_broadcast([P, 4, E])
                for k in range(TOPK):
                    top = TOP[:, k, :]
                    link(nc.vector.tensor_reduce(top, LOGIT[:], AX.X, ALU.max))
                    link(nc.vector.tensor_tensor(R1[:], LOGIT[:], top.unsqueeze(2).to_broadcast([P, 4, E]), ALU.is_equal))
                    link(nc.vector.tensor_tensor(R1[:], R1[:], rev, ALU.mult))
                    link(nc.vector.tensor_reduce(CODE[:, k, :], R1[:], AX.X, ALU.max))
                    link(nc.vector.tensor_tensor(R1[:], rev, CODE[:, k, :].unsqueeze(2).to_broadcast([P, 4, E]), ALU.is_equal))
                    if k == 0:
                        link(nc.vector.scalar_tensor_tensor(out=LOGIT[:], in0=R1[:], scalar=-3e38, in1=LOGIT[:], op0=ALU.mult, op1=ALU.add))
                    if k == 0:
                        nc.vector.tensor_copy(OH[:, :, k, :], R1[:])
                    else:
                        nc.vector.tensor_copy(OH[:, :, k, :], R1[:]).then_inc(oh_ready, 1)
                nc.vector.tensor_tensor(DELTA[:], TOP[:, 1, :], TOP[:, 0, :], ALU.subtract).then_inc(delta_ready, 1)
                assert n[0] == 11

            def place(r):
                n = [11]

                def link(ins):
                    n[0] += 1
                    ins.then_inc(route_step, 1)
                    dve.wait_ge(route_step, ROUTE * r + n[0])

                tile = 4 * r
                wait(dve, sent, 128 * r)
                dve.wait_ge(expd_ready, r + 1)
                link(nc.vector.tensor_scalar(DEN[:], EXPD[:], 1.0, None, ALU.add))
                nc.vector.reciprocal(ROWS[:, :, D], DEN[:])
                oh = OH[:].rearrange("p t k e -> p t (k e)")
                base = C[:, C_BASE:C_TRASH].unsqueeze(1).to_broadcast([P, 4, TOPK * E])
                link(nc.vector.tensor_tensor(R2[:], oh, base, ALU.mult))
                nc.vector.tensor_tensor(ROWS[:, :, D + 1], EXPD[:], ROWS[:, :, D], ALU.mult)
                nc.vector.tensor_copy(ROWS[:, :, D + 2], C[:, bass.ds(tile + C_TOKEN, 4)])
                link(nc.vector.tensor_reduce(SB[:], R2[:].rearrange("p t (k e) -> p t k e", k=TOPK), AX.X, ALU.add))
                dve.wait_ge(rk_full, r + 1)
                link(nc.vector.tensor_tensor(R2[:], M1[:, 0:4 * TOPK * E].rearrange("p (t n) -> p t n", t=4), oh, ALU.mult))
                nc.vector.tensor_reduce(ADDED[:], OH[:].rearrange("p t k e -> p (k e) t"), AX.X, ALU.add)
                link(nc.vector.tensor_reduce(RK[:], R2[:].rearrange("p t (k e) -> p t k e", k=TOPK), AX.X, ALU.add))
                nc.vector.tensor_tensor(SEENF[:], SEENF[:], ADDED[:], ALU.add)
                nc.vector.tensor_scalar(OKAY[:], RK[:], float(CAP), None, ALU.is_lt)
                link(nc.vector.tensor_tensor(SLOTF[:], SB[:], RK[:], ALU.add))
                nc.vector.tensor_copy(SEEN[:], SEENF[:])
                spare = C[:, bass.ds(2 * tile + C_TRASH, 4 * TOPK)].rearrange("p (t k) -> p t k", k=TOPK)
                link(nc.vector.tensor_tensor(SLOTF[:], SLOTF[:], spare, ALU.subtract))
                link(nc.vector.tensor_tensor(SLOTF[:], SLOTF[:], OKAY[:], ALU.mult))
                nc.vector.tensor_tensor(SLOT[:].rearrange("p (t k) -> p t k", k=TOPK), SLOTF[:], spare, ALU.add).then_inc(routed, 1)
                assert n[0] == ROUTE

            def step(it, off):
                nxt, cur, prev, prev2 = present(it, off)
                i, u = 2 * it + off, off % 2
                if cur:
                    row_max(it, off, 0)
                if prev2:
                    dve.wait_ge(rstd2_ready, i - 1)
                    wait(dve, x2t_ready, i - 3)
                    wait(dve, rows_ready, it + (off - 2) // 2)
                    for t in range(2):
                        ins = nc.vector.tensor_scalar(
                            RN[u][:, t, :], X[:, bass.ds(2 * i + (t - 4), 1), :].rearrange("p a d -> p (a d)"),
                            MV2[u][:, t, 0:1], RSTD2[u][:, t:t + 1], ALU.subtract, ALU.mult)
                    ins.then_inc(rn_ready, 1)
                if nxt:
                    dve.wait_ge(xth_ready, i + 2)
                    nc.vector.tensor_tensor(XT_LO[1 - u][:], M0[:, 0:LQ], XT_HI[1 - u][:].bitcast(F32), ALU.subtract).then_inc(xtl_ready, 1)
                if cur:
                    row_max(it, off, 1)
                if prev2:
                    dve.wait_ge(lg_full, i - 1)
                    nc.vector.tensor_copy(LOGIT[:, 2 * u:2 * u + 2, :], M1[:, 0:2 * E].rearrange("p (t e) -> p t e", e=E)
                                          ).then_inc(logit_ready, 1)
                    if u == 1:
                        dve.wait_ge(logit_ready, i - 1)
                        choose(it + (off - 3) // 2)
                if nxt:
                    queries_lo(it, off, 0)
                if prev:
                    dve.wait_ge(pv_full, i)
                    nc.vector.reciprocal(RDEN[1 - u][:], OD[:, LQ:2 * LQ]).then_inc(rden_ready, 1)
                    dve.wait_ge(rden_ready, i)
                    nc.vector.tensor_tensor(AT[1 - u][:], OD[:, 0:LQ], RDEN[1 - u][:], ALU.mult).then_inc(at_ready, 1)
                if nxt:
                    queries_lo(it, off, 1)
                if prev:
                    dve.wait_ge(wo_full, i)
                    xv = X[:, bass.ds(2 * i - 2, 2), :]
                    nc.vector.tensor_tensor(xv, M1[:, 0:2 * D].rearrange("p (t d) -> p t d", t=2), xv, ALU.add).then_inc(x1_ready, 1)
                    dve.wait_ge(x_in, 64)
                    dve.wait_ge(x1_ready, i)
                    for t in range(2):
                        ins = nc.vector.bn_stats(STATS2[1 - u][:, t, :], X[:, bass.ds(2 * i + (t - 2), 1), :].rearrange("p a d -> p (a d)"))
                    ins.then_inc(ln2_step, 1)
                    dve.wait_ge(x_in, 64)
                    dve.wait_ge(ln2_step, 2 * i - 1)
                    for t in range(2):
                        ins = nc.vector.bn_aggr(MV2[1 - u][:, t, :], STATS2[1 - u][:, t, :])
                    ins.then_inc(ln2_step, 1)
                    dve.wait_ge(ln2_step, 2 * i)
                    nc.vector.tensor_scalar(VE2[1 - u][:], MV2[1 - u][:, :, 1], EPS, None, ALU.add).then_inc(ve2_ready, 1)
                if not isinstance(it, int) or 0 <= off and off + 2 < B:
                    norm(2 * it + (off + 2), u)
                if u == 1 and prev2:
                    place(it + (off - 3) // 2)

            over_batches(dve, step)

            def slots_lo(tn, v):
                for c, (t0, nt) in enumerate(CHUNKS):
                    cols = slice(t0 * P, (t0 + nt) * P)
                    dve.wait_ge(ex_hi_ready, tn + (c + 1))
                    nc.vector.tensor_tensor(EX_LO[v][:, cols], TB[(3 * v + c) % 2][:, 0:nt * P], EX_HI[v][:, cols].bitcast(F32),
                                            ALU.subtract).then_inc(ex_ready, 1)

            def tokens_of(v, loads):
                dve.wait_ge(xl_in[v], 16 * loads)
                nc.vector.tensor_copy(IDX[v][:], XL[v][:, :, D + 2]).then_inc(idx_ready, 1)

            def weigh(it, n, v):
                t0, nt = CHUNKS[n % 3]
                dve.wait_ge(dn_full, 6 * it + (n + 1))
                wait(dve, returned[n % 2], 160 * it + 16 * RETURNS[n][n % 2])
                for t in range(nt):
                    k = (t0 + t) * P // CAP
                    ins = nc.vector.tensor_scalar(YS[n % 2][:, t, :], Y_PS[n % 2][:, t * D:(t + 1) * D],
                                                  XL[v][:, t0 + t, D + k:D + k + 1], None, ALU.mult)
                ins.then_inc(y_ready, 1)

            slots_lo(0, 0)
            tokens_of(0, 1)

            def pair(it, last):
                for v in range(2):
                    for c, (t0, nt) in enumerate(CHUNKS):
                        n = 3 * v + c
                        for f in range(FT):
                            m = 4 * n + f
                            dve.wait_ge(sg_ready, 24 * it + (m + 1))
                            if f == 0:
                                wait(dve, dn_full, 6 * it + (n - 1))
                            nc.vector.tensor_tensor(H[n % 2][:, f, 0:nt * P], SG[m % 2][:, 0:nt * P], UP_PS[m % 2][:, 0:nt * P],
                                                    ALU.mult).then_inc(h_ready, 1)
                            if f == 2 and c > 0:
                                weigh(it, n - 1, v)
                    if not (last and v == 1):
                        slots_lo(6 * it + (3 * v + 3), 1 - v)
                    weigh(it, 3 * v + 2, v)
                    if not (last and v == 1):
                        for w in range(2):
                            wait(dve, returned[w], 160 * it + 16 * RETURNS[3 * v][w])
                        tokens_of(1 - v, it + (v + 1))

            over_experts(dve, pair)
            for q in range(4):
                dve.wait_ge(fb_in[q], 32)
                xv = X[:, 8 * q:8 * q + 8, :]
                nc.vector.tensor_tensor(FB[0][q][:], FB[0][q][:], FB[1][q][:], ALU.add).then_inc(add_step, 1)
                dve.wait_ge(add_step, q + 1)
                nc.vector.tensor_tensor(xv, xv, FB[0][q][:], ALU.add).then_inc(out_ready, 1)


def kernel(**inputs):
    import concourse.bacc as bacc
    from concourse.bass_utils import run_bass_kernel_spmd

    a = {k: np.asarray(v) for k, v in inputs.items()}
    const, empty, zeros = constants()

    def stacked(w):
        g = w.reshape(D, GROUPS, 1, 32)
        return np.ascontiguousarray(np.broadcast_to(g, (D, GROUPS, 3, 32)).reshape(D, GROUPS, 96))

    ctx = a["ctx_1024"].transpose(2, 0, 1)[:, :, None, :]
    wg, wu, wd = (a["L0_ffn_" + n] for n in ("wi_gate", "wi_up", "wo"))
    arrays = {
        "x": np.ascontiguousarray(a["x"].reshape(TOKENS, D)),
        "ctx": np.ascontiguousarray(np.broadcast_to(ctx, (D, B, 2, LK))),
        "mask": np.ascontiguousarray(a["mask_BxS2_ik0"]),
        "wq": stacked(a["L0_xattn_Wq"]),
        "wk": stacked(a["L0_xattn_Wk"]),
        "wv": a["L0_xattn_Wv"],
        "wo": a["L0_xattn_Wo"],
        "gate": np.ascontiguousarray(a["L0_ffn_gate_w"].T),
        "wgu": np.ascontiguousarray(np.concatenate([wg.transpose(0, 2, 1), wu.transpose(0, 2, 1)], axis=2)),
        "wdn": np.ascontiguousarray(wd.transpose(0, 2, 1).reshape(E, FT, P, D).transpose(0, 2, 1, 3).reshape(E, P, FT * D)),
        "const": const,
        "empty": empty,
        "zeros": zeros,
    }
    nc = bacc.Bacc("TRN2", target_bir_lowering=False, num_devices=1)
    args = [nc.dram_tensor(f"in_{n}", v.shape, mybir.dt.from_np(v.dtype), kind="ExternalInput").ap() for n, v in arrays.items()]
    args.append(nc.dram_tensor("out", (TOKENS, D), F32, kind="ExternalOutput").ap())
    program(nc, *args)
    r = run_bass_kernel_spmd(nc, [{f"in_{n}": v for n, v in arrays.items()}], core_ids=[0])
    return r.results[0]["out"].reshape(B, LQ, D)
```

```python
from contextlib import ExitStack

import concourse.bass as bass
import numpy as np
from concourse import mybir

F32 = mybir.dt.float32
F32R = mybir.dt.float32r
BF16 = mybir.dt.bfloat16
I32 = mybir.dt.int32
ALU = mybir.AluOpType
ACT = mybir.ActivationFunctionType
AX = mybir.AxisListType

P = 128
B, LQ, LK, D = 16, 256, 64, 128
HEADS, DPH = 16, 8
GROUPS, HG = 4, 4
TOKENS = B * LQ
TILES = TOKENS // P
E, F, TOPK = 8, 512, 2
CAP = int(TOKENS / E * 1.25)
ESLOTS = TOPK * CAP
SLOTS = E * ESLOTS
STILES = ESLOTS // P
ROW = 132
EPS = 1e-5
BIG = float(2.0 ** 127)
SCALE = DPH ** -0.5
ONE_ROW = 96
NROW = ONE_ROW + 1 + HEADS
FT = F // P
CHUNKS = [(0, 4), (4, 3), (7, 3)]

C_IDENT = 0
C_KMASK = C_IDENT + P
C_VMASK = C_KMASK + GROUPS * HG
C_REV = C_VMASK + 2 * P
C_BASE = C_REV + E
C_TRASH = C_BASE + TOPK * E
C_TOKEN = C_TRASH + TILES * TOPK
C_TRI = C_TOKEN + TILES
NCONST = C_TRI + P


def constants():
    c = np.zeros((P, NCONST), np.float32)
    p = np.arange(P)
    c[:, C_IDENT:C_IDENT + P] = np.eye(P)
    km = np.zeros((P, GROUPS, HG), np.float32)
    for r in range(ONE_ROW):
        km[r, :, (r % 32) // DPH] = 1
    km[ONE_ROW] = 1
    for h in range(HEADS):
        km[ONE_ROW + 1 + h, h // HG, h % HG] = 1
    c[:, C_KMASK:C_VMASK] = km.reshape(P, -1)
    vm = np.zeros((P, 2, GROUPS, HG, DPH), np.float32)
    for s in range(2):
        for half in range(2):
            vm[64 * half:64 * half + 64, s, :, 2 * s + half, :] = 1
    c[:, C_VMASK:C_REV] = vm.reshape(P, -1)
    c[:, C_REV:C_BASE] = E - np.arange(E)
    c[:, C_BASE:C_TRASH] = (np.arange(E)[None, :] * ESLOTS + np.arange(TOPK)[:, None] * CAP).reshape(-1)
    token = np.arange(TILES)[None, :] * P + p[:, None]
    c[:, C_TRASH:C_TOKEN] = (SLOTS + token[:, :, None] + TOKENS * np.arange(TOPK)).reshape(P, -1)
    c[:, C_TOKEN:C_TRI] = token
    c[:, C_TRI:] = p[:, None] < p[None, :]
    empty = np.zeros((ESLOTS, ROW), np.float32)
    empty[:, 130] = TOKENS + np.arange(ESLOTS)
    return c, empty, np.zeros((1024, D), np.float32)


def program(nc, x, ctx, mask, wq, wk, wv, wo, gate, wgu, wdn, const, empty, zeros, out):
    slots = nc.dram_tensor("slots", [SLOTS + TOPK * TOKENS, ROW], F32, kind="Internal").ap()
    back = [nc.dram_tensor(f"back{k}", [TOKENS + ESLOTS, D], F32, kind="Internal").ap() for k in range(TOPK)]
    x_t = x.rearrange("(t p) d -> p t d", p=P)
    out_t = out.rearrange("(t p) d -> p t d", p=P)

    with ExitStack() as stack:
        def sb(name, shape, dt=F32, where=stack):
            return where.enter_context(nc.sbuf_tensor(name, shape, dt))

        def sem(name):
            return stack.enter_context(nc.semaphore(name))

        X = sb("X", [P, TILES, D])
        C = sb("C", [P, NCONST])
        W_RAW = [sb(f"w_raw{v}", [P, 2 * F + FT * D]) for v in range(2)]
        W_HI = [sb(f"w_hi{v}", [P, 2 * F], F32R) for v in range(2)]
        W_LO = [sb(f"w_lo{v}", [P, 2 * F], F32R) for v in range(2)]
        XL = [sb(f"xl{v}", [P, STILES, ROW]) for v in range(2)]
        IDX = [sb(f"idx{v}", [P, STILES], I32) for v in range(2)]
        part1 = ExitStack()

        def s1(name, shape, dt=F32):
            return sb(name, shape, dt, part1)

        TRI = s1("tri", [P, P], BF16)
        ONES = s1("ones", [P, P], BF16)
        CTX = s1("ctx", [P, B, 2, LK])
        CTXM = s1("ctxm", [P, B, LK])
        CTX_HI = s1("ctx_hi", [P, B * LK], F32R)
        CTX_LO = s1("ctx_lo", [P, B * LK], F32R)
        MASKI = s1("maski", [P, B, LK], I32)
        MASKF = s1("maskf", [P, B, LK])
        ANY = s1("any", [P, B])
        NW = D + GROUPS * 96
        WQK = s1("wqk", [P, NW])
        WQK_HI = s1("wqk_hi", [P, NW], F32R)
        WQK_LO = s1("wqk_lo", [P, NW], F32R)
        SEL_HI = s1("sel_hi", [P, GROUPS, 3, 32], F32R)
        SEL_LO = s1("sel_lo", [P, GROUPS, 3, 32], F32R)
        WV = s1("wv", [P, D])
        WO = s1("wo", [P, D])
        GATE = s1("gate", [P, E])
        KC = s1("kc", [P, B, GROUPS, LK])
        VALL = s1("vall", [P, B, D])
        STATS = s1("stats", [P, TILES, 6])
        MV = s1("mv", [P, TILES, 2])
        VE = s1("ve", [P, TILES])
        RSTD = s1("rstd", [P, TILES])
        HALF = s1("half", [P, TILES])
        XN = [s1(f"xn{v}", [P, 2, D]) for v in range(2)]
        XT_HI = [s1(f"xt_hi{v}", [P, LQ], F32R) for v in range(2)]
        XT_LO = [s1(f"xt_lo{v}", [P, LQ], F32R) for v in range(2)]
        Q_HI = s1("q_hi", [P, LQ], F32R)
        Q_LO = s1("q_lo", [P, LQ], F32R)
        QS = [s1(f"qs{v}", [P, GROUPS, LQ], F32R) for v in range(2)]
        KS = [s1(f"ks{v}", [P, GROUPS, HG * LK], F32R) for v in range(2)]
        V2 = [s1(f"v2{v}", [P, 2, GROUPS, 32]) for v in range(2)]
        MNEG = [s1(f"mneg{v}", [P, 2, 1 + HEADS]) for v in range(2)]
        PROBS = [s1(f"probs{v}", [P, GROUPS, 2, LQ]) for v in range(2)]
        LOGD = s1("logd", [P, LQ])
        GUESS = s1("guess", [P, LQ])
        ERR = s1("err", [P, LQ])
        RNEG = s1("rneg", [P, LQ])
        AT = s1("at", [P, LQ])
        STATS2 = [s1(f"stats2{v}", [P, 2, 6]) for v in range(2)]
        MV2 = [s1(f"mv2{v}", [P, 2, 2]) for v in range(2)]
        VE2 = [s1(f"ve2{v}", [P, 2]) for v in range(2)]
        RSTD2 = [s1(f"rstd2{v}", [P, 2]) for v in range(2)]
        RALL = s1("rall", [P, TILES, ROW])
        RN = [s1(f"rn{v}", [P, 2, D]) for v in range(2)]
        X2T = [s1(f"x2t{v}", [P, LQ]) for v in range(2)]
        ROWS = [s1(f"rows{v}", [P, 2, ROW]) for v in range(2)]
        LOGIT = s1("logit", [P, 4, E])
        LOGIT2 = s1("logit2", [P, 4, E])
        R1 = s1("r1", [P, 4, E])
        R2 = s1("r2", [P, 4, TOPK * E])
        R3 = s1("r3", [P, 4, TOPK * E])
        TOP = s1("top", [P, TOPK, 4])
        CODE = s1("code", [P, TOPK, 4])
        OH = s1("oh", [P, 4, TOPK, E], BF16)
        SEEN = s1("seen", [P, TOPK * E], BF16)
        SEENF = s1("seenf", [P, TOPK * E])
        ADDED = s1("added", [P, TOPK * E])
        DELTA = s1("delta", [P, 4])
        EXPD = s1("expd", [P, 4])
        DEN = s1("den", [P, 4])
        RK = s1("rk", [P, 4, TOPK])
        SB = s1("sb", [P, 4, TOPK])
        OKAY = s1("okay", [P, 4, TOPK])
        SLOTF = s1("slotf", [P, 4, TOPK])
        SLOT = [s1(f"slot{v}", [P, 2 * TOPK], I32) for v in range(2)]
        part1.close()
        part2 = ExitStack()

        def s2(name, shape, dt=F32):
            return sb(name, shape, dt, part2)

        EX_HI = [s2(f"ex_hi{v}", [P, ESLOTS], F32R) for v in range(2)]
        EX_LO = [s2(f"ex_lo{v}", [P, ESLOTS], F32R) for v in range(2)]
        SG = [s2(f"sg{v}", [P, 512]) for v in range(2)]
        H = [s2(f"h{v}", [P, FT, 512]) for v in range(2)]
        YS = [s2(f"ys{v}", [P, 4, D]) for v in range(2)]
        part2.close()
        part3 = ExitStack()
        FB = [[sb(f"fb{k}{q}", [P, 8, D], F32, part3) for q in range(4)] for k in range(TOPK)]
        part3.close()

        BANK = [stack.enter_context(nc.psum_tensor(f"bank{i}", [P, 512], F32)) for i in range(8)]
        MX, ST, QP, DEN_PS, M0, M1 = BANK[0:2], BANK[2:4], BANK[4], BANK[5], BANK[6], BANK[7]
        OUT_PS = ST[1]
        GATE_PS, UP_PS, TB, Y_PS = BANK[0:2], BANK[2:4], BANK[4:6], BANK[6:8]

        const_in, x_in, mask_in, ctx_in, w_in = sem("const_in"), sem("x_in"), sem("mask_in"), sem("ctx_in"), sem("w_in")
        ext_in = sem("ext_in")
        filled = sem("filled")
        raw_in = [sem(f"raw_in{v}") for v in range(2)]
        setup = sem("setup")
        wsplit = sem("wsplit")
        ctx_split = sem("ctx_split")
        pool_setup = sem("pool_setup")
        k_full, k_hi, k_used = sem("k_full"), sem("k_hi"), sem("k_used")
        v_full, v_used = sem("v_full"), sem("v_used")
        ve_ready, rstd_ready = sem("ve_ready"), sem("rstd_ready")
        xn_ready, tx_full, xth_ready, xtl_ready = sem("xn_ready"), sem("tx_full"), sem("xth_ready"), sem("xtl_ready")
        q_full, qhi_ready, qlo_ready = sem("q_full"), sem("qhi_ready"), sem("qlo_ready")
        sel_full, qs_ready = sem("sel_full"), sem("qs_ready")
        ks_ready, v2_ready = sem("ks_ready"), sem("v2_ready")
        mx_full, m_ready, mt_full, aug_ready = sem("mx_full"), sem("m_ready"), sem("mt_full"), sem("aug_ready")
        st_full, p_ready, den_full, pv_full = sem("st_full"), sem("p_ready"), sem("den_full"), sem("pv_full")
        logd_ready, guess_ready, newton_step = sem("logd_ready"), sem("guess_ready"), sem("newton_step")
        at_ready, wo_full, x1_ready = sem("at_ready"), sem("wo_full"), sem("x1_ready")
        ln2_step, ve2_ready, rstd2_ready, rn_ready = sem("ln2_step"), sem("ve2_ready"), sem("rstd2_ready"), sem("rn_ready")
        tx2_full, x2t_ready, lg_full, logit_ready = sem("tx2_full"), sem("x2t_ready"), sem("lg_full"), sem("logit_ready")
        route_step = sem("route_step")
        oh_ready, rk_full, delta_ready, expd_ready = sem("oh_ready"), sem("rk_full"), sem("delta_ready"), sem("expd_ready")
        rk_used, slot_ready, rows_ready = sem("rk_used"), sem("slot_ready"), sem("rows_ready")
        rows_kept = sem("rows_kept")
        sent = [sem(f"sent{v}") for v in range(2)]
        xl_in = [sem(f"xl_in{v}") for v in range(2)]
        w_hi_ready, w_ready = sem("w_hi_ready"), sem("w_ready")
        tb_full, ex_hi_ready, ex_ready, idx_ready = sem("tb_full"), sem("ex_hi_ready"), sem("ex_ready"), sem("idx_ready")
        g_full, u_full = sem("g_full"), sem("u_full")
        sg_ready, h_ready, dn_full, y_ready = sem("sg_ready"), sem("h_ready"), sem("dn_full"), sem("y_ready")
        returned = [sem(f"returned{v}") for v in range(2)]
        fb_in = [sem(f"fb_in{q}") for q in range(4)]
        add_step, out_ready, stored = sem("add_step"), sem("out_ready"), sem("stored")

        IDENT = C[:, C_IDENT:C_IDENT + P]
        KMASK = C[:, C_KMASK:C_VMASK]
        VMASK = C[:, C_VMASK:C_REV].rearrange("p (s g c) -> p s g c", s=2, g=GROUPS)

        def over_batches(eng, step):
            for i in range(-1, 8):
                step(0, i)
            with eng.Fori(4, 7) as it:
                step(it, 0)
                step(it, 1)
            for i in range(14, B + 6):
                step(0, i)

        def has(it, off, ahead):
            return not isinstance(it, int) or 0 <= off + ahead < B

        def wait(eng, s, value):
            if not isinstance(value, int) or value > 0:
                eng.wait_ge(s, value)

        def held(eng, value):
            return value if isinstance(value, int) else eng.to_reg(value)

        def over_experts(eng, pair):
            pair(0, False)
            with eng.Fori(1, E // 2 - 1) as it:
                pair(it, False)
            pair(E // 2 - 1, True)

        RETURNS = [[sum(CHUNKS[m % 3][1] for m in range(n) if m % 2 == w) for w in range(2)] for n in range(7)]

        block = stack.enter_context(nc.Block())

        @block.sync
        def _(sp):
            sp.dma_start(C[:], const).then_inc(const_in, 16)
            sp.dma_start(MASKI[:].rearrange("p b k -> p (b k)"),
                         mask.rearrange("b k -> (b k)").rearrange("(a n) -> a n", a=1).to_broadcast([P, B * LK])
                         ).then_inc(mask_in, 16)
            sp.dma_start(CTX[:], ctx).then_inc(ctx_in, 16)
            sp.dma_start(WQK[:, 0:D], wq).then_inc(w_in, 16)
            sp.dma_start(WQK[:, D:], wk).then_inc(w_in, 16)
            sp.dma_start(WV[:], wv).then_inc(w_in, 16)
            sp.dma_start(WO[:], wo).then_inc(w_in, 16)
            sp.dma_start(GATE[:], gate).then_inc(w_in, 16)
            sp.wait_ge(setup, 5)
            sp.wait_ge(pool_setup, 1)
            for g in range(GROUPS):
                sp.dma_start(KC[ONE_ROW:ONE_ROW + 1, :, g, :], MASKF[ONE_ROW:ONE_ROW + 1]).then_inc(ext_in, 16)
            for e in range(E):
                sp.dma_start(slots[e * ESLOTS:(e + 1) * ESLOTS, :], empty).then_inc(filled, 16)
            for k in range(TOPK):
                for q in range(TOKENS // 1024):
                    sp.dma_start(back[k][q * 1024:(q + 1) * 1024, :], zeros).then_inc(filled, 16)
            for v in range(2):
                sp.dma_start(W_RAW[v][:, 0:2 * F], wgu[v]).then_inc(raw_in[v], 16)
                sp.dma_start(W_RAW[v][:, 2 * F:], wdn[v]).then_inc(raw_in[v], 16)
            for v in range(2):
                sp.wait_ge(sent[v], 64 * (B // 2))
            for v in range(2):
                sp.dma_start(XL[v][:], slots[v * ESLOTS:(v + 1) * ESLOTS, :].rearrange("(t p) c -> p t c", p=P)
                             ).then_inc(xl_in[v], 16)

            def pair(it, last):
                for v in range(2):
                    if last:
                        continue
                    sp.wait_ge(y_ready, 6 * it + 3 * v + 3)
                    e = 2 * it + (v + 2)
                    sp.dma_start(W_RAW[v][:, 0:2 * F], wgu[bass.ds(e, 1)].rearrange("a p f -> (a p) f")).then_inc(raw_in[v], 16)
                    sp.dma_start(W_RAW[v][:, 2 * F:], wdn[bass.ds(e, 1)].rearrange("a p f -> (a p) f")).then_inc(raw_in[v], 16)
                    sp.dma_start(XL[v][:], slots[bass.ds(e * ESLOTS, ESLOTS), :].rearrange("(t p) c -> p t c", p=P)
                                 ).then_inc(xl_in[v], 16)

            over_experts(sp, pair)
            for v in range(2):
                sp.wait_ge(returned[v], 16 * 10 * (E // 2))
            for q in range(4):
                for k in range(TOPK):
                    sp.dma_start(FB[k][q][:], back[k][q * 1024:(q + 1) * 1024, :].rearrange("(t p) d -> p t d", p=P)
                                 ).then_inc(fb_in[q], 16)
            for q in range(4):
                sp.wait_ge(out_ready, q + 1)
                sp.dma_start(out_t[:, 8 * q:8 * q + 8, :], X[:, 8 * q:8 * q + 8, :]).then_inc(stored, 16)
            sp.wait_ge(stored, 64)

        @block.gpsimd
        def _(pool):
            nc.gpsimd.memset(KC[ONE_ROW:, :, :, :], 1.0).then_inc(pool_setup, 1)
            pool.wait_ge(pool_setup, 1)
            nc.gpsimd.memset(HALF[:], -0.5).then_inc(pool_setup, 1)
            pool.wait_ge(pool_setup, 2)
            pool.wait_ge(ve_ready, 1)
            nc.gpsimd.tensor_tensor(RSTD[:], VE[:], HALF[:], ALU.pow).then_inc(rstd_ready, 1)
            pool.wait_ge(const_in, 16)
            nc.gpsimd.memset(SEL_HI[:, :, 1, :].bitcast(F32), 0.0)
            nc.gpsimd.memset(SEL_LO[:].bitcast(F32), 0.0).then_inc(pool_setup, 1)
            pool.wait_ge(pool_setup, 3)
            ident_g = IDENT.rearrange("p (g c) -> p g c", g=GROUPS)
            for part, sel in ((0, SEL_HI), (2, SEL_HI), (1, SEL_LO)):
                ins = nc.gpsimd.tensor_copy(sel[:, :, part, :], ident_g)
            ins.then_inc(pool_setup, 1)
            pool.wait_ge(const_in, 16)
            pool.wait_ge(k_used, 8)
            pool.wait_ge(ext_in, 64)
            pool.wait_ge(v_used, 4)

            def spread_keys(it, off, c):
                i = 2 * it + (off + c)
                v = (off + c) % 2
                wait(pool, st_full, 4 * i - 4)
                nc.gpsimd.tensor_tensor(
                    KS[v][0:NROW].rearrange("p g (h k) -> p g h k", h=HG),
                    KC[0:NROW, bass.ds(i, 1)].rearrange("p a g k -> p (a g) k").unsqueeze(2).to_broadcast([NROW, GROUPS, HG, LK]),
                    KMASK[0:NROW].rearrange("p (g h) -> p g h", g=GROUPS).unsqueeze(3).to_broadcast([NROW, GROUPS, HG, LK]),
                    ALU.mult).then_inc(ks_ready, 1)

            def spread_values(it, off):
                i = 2 * it + off
                wait(pool, pv_full, i - 1)
                nc.gpsimd.tensor_tensor(
                    V2[off % 2][:].rearrange("p s g c -> p s (g c)"),
                    VALL[:, bass.ds(i, 1), :].to_broadcast([P, 2, D]),
                    VMASK.rearrange("p s g c -> p s (g c)"), ALU.mult).then_inc(v2_ready, 1)

            def send(it, off, t):
                u = off % 2
                for k in range(TOPK):
                    nc.gpsimd.indirect_dma_start(
                        out=slots[:, :], out_offset=bass.IndirectOffsetOnAxis(ap=SLOT[u][:, TOPK * t + k:TOPK * t + k + 1], axis=0),
                        in_=ROWS[u][:, t, :], in_offset=None).then_inc(sent[u], 16)

            def step(it, off):
                i, u = 2 * it + off, off % 2
                if has(it, off, -2):
                    wait(pool, ve2_ready, i - 1)
                    nc.gpsimd.tensor_tensor(RSTD2[u][:], VE2[u][:], HALF[:, 0:2], ALU.pow).then_inc(rstd2_ready, 1)
                if has(it, off, -6):
                    ready = held(pool, i - 5)
                    pool.wait_ge(filled, 16 * (E + TOPK * TOKENS // 1024))
                    pool.wait_ge(slot_ready, ready)
                    pool.wait_ge(rows_ready, ready)
                    send(it, off, 0)
                if has(it, off, 1):
                    spread_keys(it, off, 1)
                if has(it, off, 0):
                    spread_values(it, off)
                if has(it, off, -6):
                    send(it, off, 1)

            over_batches(pool, step)

            def split_weights(e, v, loads):
                loaded, used = held(pool, 32 * loads), held(pool, 12 * e - 12)
                pool.wait_ge(const_in, 16)
                pool.wait_ge(raw_in[v], loaded)
                wait(pool, u_full, used)
                nc.gpsimd.tensor_copy(W_HI[v][:], W_RAW[v][:, 0:2 * F]).then_inc(w_hi_ready, 1)
                pool.wait_ge(w_hi_ready, e + 1)
                nc.gpsimd.tensor_tensor(W_LO[v][:], W_RAW[v][:, 0:2 * F], W_HI[v][:].bitcast(F32), ALU.subtract
                                        ).then_inc(w_ready, 1)

            split_weights(0, 0, 1)

            def pair(it, last):
                for v in range(2):
                    if not (last and v == 1):
                        split_weights(2 * it + (v + 1), 1 - v, it + (v + 1))
                    for c, (t0, nt) in enumerate(CHUNKS):
                        n = 3 * v + c
                        rows = held(pool, 6 * it + (n + 1))
                        pool.wait_ge(filled, 16 * (E + TOPK * TOKENS // 1024))
                        pool.wait_ge(y_ready, rows)
                        for t in range(nt):
                            j = t0 + t
                            nc.gpsimd.indirect_dma_start(
                                out=back[j * P // CAP][:, :],
                                out_offset=bass.IndirectOffsetOnAxis(ap=IDX[v][:, j:j + 1], axis=0),
                                in_=YS[n % 2][:, t, :], in_offset=None).then_inc(returned[n % 2], 16)

            over_experts(pool, pair)
            for v in range(2):
                pool.wait_ge(returned[v], 16 * 10 * (E // 2))

        @block.scalar
        def _(act):
            nc.scalar.preload_act_table_set("natural_log_exp_and_others")
            for q in range(4):
                act.dma_start(X[:, 8 * q:8 * q + 8, :], x_t[:, 8 * q:8 * q + 8, :]).then_inc(x_in, 16)
            act.wait_ge(w_in, 80)
            nc.scalar.copy(WQK_HI[:], WQK[:]).then_inc(wsplit, 1)
            act.wait_ge(setup, 3)
            nc.scalar.copy(CTX_HI[:], CTXM[:].rearrange("p b k -> p (b k)")).then_inc(ctx_split, 1)
            for n in range(8):
                g, half = n // 2, n % 2
                act.wait_ge(k_full, n + 1)
                nc.scalar.copy(KC[0:96, 8 * half:8 * half + 8, g, :].bitcast(F32R),
                               MX[n % 2][0:96, :].rearrange("p (b k) -> p b k", k=LK)).then_inc(k_hi, 1)
            for n in range(4):
                act.wait_ge(v_full, n + 1)
                nc.scalar.copy(VALL[:, 4 * n:4 * n + 4, :], ST[n % 2][:].rearrange("p (b d) -> p b d", d=D)).then_inc(v_used, 1)

            def exps(it, off, c, j):
                i = 2 * it + (off + c)
                act.wait_ge(st_full, 4 * i + (j + 1))
                if j == 0:
                    wait(act, pv_full, i - 1)
                nc.scalar.activation(PROBS[(off + c) % 2][:, j].rearrange("p s q -> p (s q)"), ST[j % 2][:], ACT.Exp
                                     ).then_inc(p_ready, 1)

            def stack_queries(it, off, h):
                i, u = 2 * it + off, off % 2
                act.wait_ge(sel_full, 2 * i + (3 + h))
                if h == 0:
                    wait(act, st_full, 4 * i)
                nc.scalar.copy(QS[1 - u][0:96, 2 * h:2 * h + 2, :].rearrange("p g q -> p (g q)"), QP[0:96, :]).then_inc(qs_ready, 1)

            def step(it, off):
                i, u = 2 * it + off, off % 2
                if u == 1 and has(it, off, -5):
                    act.wait_ge(delta_ready, it + ((off - 5) // 2 + 1))
                    nc.scalar.activation(EXPD[:], DELTA[:], ACT.Exp).then_inc(expd_ready, 1)
                if has(it, off, 1):
                    act.wait_ge(tx_full, i + 2)
                    wait(act, q_full, i)
                    nc.scalar.copy(XT_HI[1 - u][:], M0[:, 0:LQ]).then_inc(xth_ready, 1)
                if has(it, off, -1):
                    exps(it, off, -1, 2)
                if has(it, off, -6):
                    act.wait_ge(slot_ready, i - 5)
                    act.wait_ge(rows_kept, i - 5)
                    wait(act, sent[u], 64 * it + 64 * ((off - 6) // 2))
                    nc.scalar.copy(ROWS[u][:], RALL[:, bass.ds(2 * i - 12, 2), :]).then_inc(rows_ready, 1)
                if has(it, off, -1):
                    exps(it, off, -1, 3)
                if has(it, off, 1):
                    act.wait_ge(q_full, i + 2)
                    nc.scalar.mul(Q_HI[:], M0[:, 0:LQ], SCALE).then_inc(qhi_ready, 1)
                if has(it, off, -2):
                    act.wait_ge(tx2_full, i - 1)
                    nc.scalar.copy(X2T[u][:], M1[:, 0:LQ]).then_inc(x2t_ready, 1)
                    nc.scalar.copy(RALL[:, bass.ds(2 * i - 4, 2), 0:D], RN[u][:]).then_inc(rows_kept, 1)
                if has(it, off, -1):
                    act.wait_ge(den_full, i)
                    nc.scalar.activation(LOGD[:], DEN_PS[:, 0:LQ], ACT.Ln).then_inc(logd_ready, 1)
                if has(it, off, 1):
                    stack_queries(it, off, 0)
                if has(it, off, -1):
                    act.wait_ge(logd_ready, i)
                    nc.scalar.activation(GUESS[:], LOGD[:], ACT.Exp, scale=-1.0).then_inc(guess_ready, 1)
                if has(it, off, 0):
                    act.wait_ge(mt_full, i + 1)
                    nc.scalar.copy(QS[u][ONE_ROW:NROW, :, :],
                                   M0[0:1 + HEADS, 0:LQ].unsqueeze(1).to_broadcast([1 + HEADS, GROUPS, LQ])).then_inc(aug_ready, 1)
                if has(it, off, 1):
                    stack_queries(it, off, 1)
                if has(it, off, 0):
                    exps(it, off, 0, 0)
                    exps(it, off, 0, 1)

            over_batches(act, step)

            def slots_hi(tn, v):
                for c, (t0, nt) in enumerate(CHUNKS):
                    act.wait_ge(tb_full, tn + (c + 1))
                    nc.scalar.copy(EX_HI[v][:, t0 * P:(t0 + nt) * P], TB[(3 * v + c) % 2][:, 0:nt * P]).then_inc(ex_hi_ready, 1)

            slots_hi(0, 0)

            def pair(it, last):
                for v in range(2):
                    for c, (t0, nt) in enumerate(CHUNKS):
                        for f in range(FT):
                            m = 12 * v + 4 * c + f
                            act.wait_ge(g_full, 24 * it + (m + 1))
                            wait(act, h_ready, 24 * it + (m - 1))
                            nc.scalar.activation(SG[m % 2][:, 0:nt * P], GATE_PS[m % 2][:, 0:nt * P], ACT.Silu).then_inc(sg_ready, 1)
                    if not (last and v == 1):
                        slots_hi(6 * it + (3 * v + 3), 1 - v)

            over_experts(act, pair)

        @block.tensor
        def _(pe):
            def product3(ps, hi, lo, m_hi, m_lo):
                nc.tensor.matmul(ps, hi, m_hi, start=True, stop=False)
                nc.tensor.matmul(ps, lo, m_hi, start=False, stop=False)
                return nc.tensor.matmul(ps, hi, m_lo, start=False, stop=True)

            pe.wait_ge(setup, 8)
            pe.wait_ge(wsplit, 2)
            pe.wait_ge(ctx_split, 2)
            for n in range(8):
                g, half = n // 2, n % 2
                if n >= 2:
                    pe.wait_ge(k_used, n - 1)
                cols = slice(512 * half, 512 * half + 512)
                product3(MX[n % 2][0:96, :], WQK_HI[:, D + 96 * g:D + 96 * g + 96], WQK_LO[:, D + 96 * g:D + 96 * g + 96], CTX_HI[:, cols], CTX_LO[:, cols]
                         ).then_inc(k_full, 1)
            for n in range(4):
                if n >= 2:
                    pe.wait_ge(v_used, n - 1)
                for b in range(4):
                    mm = nc.tensor.matmul(ST[n % 2][:, b * D:(b + 1) * D], CTX[:, 4 * n + b].rearrange("p a k -> p (a k)"), WV[:],
                                          start=True, stop=True)
                mm.then_inc(v_full, 1)
            pe.wait_ge(k_used, 8)
            pe.wait_ge(v_used, 4)
            pe.wait_ge(pool_setup, 4)

            def row_scores(it, off, m):
                i, u = 2 * it + off, off % 2
                t, b = m // 2, m % 2
                if m == 0:
                    pe.wait_ge(qs_ready, 2 * i + 2)
                    pe.wait_ge(ks_ready, i + 1)
                wait(pe, m_ready, 4 * i + (m - 1))
                for gg in range(2):
                    g = 2 * b + gg
                    mm = nc.tensor.matmul(MX[b][:, gg * HG * LK:(gg + 1) * HG * LK],
                                          QS[u][0:ONE_ROW + 1, g, t * P:(t + 1) * P], KS[u][0:ONE_ROW + 1, g, :],
                                          start=True, stop=True)
                mm.then_inc(mx_full, 1)

            def scores(it, off, c, j):
                i, u = 2 * it + (off + c), (off + c) % 2
                if j == 0:
                    pe.wait_ge(aug_ready, i + 1)
                wait(pe, p_ready, 4 * i + (j - 1))
                for s in range(2):
                    mm = nc.tensor.matmul(ST[j % 2][:, s * LQ:(s + 1) * LQ], KS[u][0:NROW, j, s * P:(s + 1) * P],
                                          QS[u][0:NROW, j, :], start=True, stop=True)
                mm.then_inc(st_full, 1)

            def select(it, off, h):
                i = 2 * it + off
                if h == 0:
                    pe.wait_ge(qlo_ready, i + 2)
                wait(pe, qs_ready, 2 * i + (2 + h))
                if h == 0 and off % 2 == 1 and has(it, off, -5):
                    pe.wait_ge(rk_used, it + ((off - 5) // 2 + 1))
                for gg in range(2):
                    g = 2 * h + gg
                    ps = QP[0:96, gg * LQ:(gg + 1) * LQ]
                    nc.tensor.matmul(ps, SEL_HI[:, g].rearrange("p a c -> p (a c)"), Q_HI[:], start=True, stop=False)
                    mm = nc.tensor.matmul(ps, SEL_LO[:, g].rearrange("p a c -> p (a c)"), Q_LO[:], start=False, stop=True)
                mm.then_inc(sel_full, 1)

            def values(it, off, what):
                v = (off + 1) % 2
                for s in range(2):
                    for g in range(GROUPS):
                        w = V2[v][:, s, g, :] if what == 0 else VMASK[:, s, g, :]
                        mm = nc.tensor.matmul((OUT_PS, DEN_PS)[what][32 * g:32 * g + 32, 0:LQ], w,
                                              PROBS[v][:, g, s, :], start=(s == 0), stop=(s == 1))
                return mm

            def step(it, off):
                i, u = 2 * it + off, off % 2
                if has(it, off, 1):
                    pe.wait_ge(xn_ready, i + 2)
                    wait(pe, qlo_ready, i + 1)
                    for t in range(2):
                        mm = nc.tensor.transpose(M0[:, t * P:(t + 1) * P], XN[1 - u][:, t, :], IDENT)
                    mm.then_inc(tx_full, 1)
                if has(it, off, 0):
                    row_scores(it, off, 0)
                if has(it, off, -1):
                    scores(it, off, -1, 2)
                if u == 1 and has(it, off, -5):
                    r = it + (off - 5) // 2
                    pe.wait_ge(oh_ready, r + 1)
                    n = TOPK * E
                    ranks = QP[:, 0:4 * n]
                    oh = OH[:].rearrange("p t k e -> p t (k e)")
                    nc.tensor.matmul(ranks, TRI[:], oh.rearrange("p t n -> p (t n)"), start=True, stop=False, skip_group_check=True)
                    for t in range(3):
                        nc.tensor.matmul(ranks[:, (t + 1) * n:], ONES[:], oh[:, t:t + 1, :].to_broadcast([P, 3 - t, n]),
                                         start=False, stop=False, skip_group_check=True)
                    nc.tensor.matmul(ranks, ONES[:], SEEN[:].unsqueeze(1).to_broadcast([P, 4, n]),
                                     start=False, stop=True, skip_group_check=True).then_inc(rk_full, 1)
                if has(it, off, -1):
                    scores(it, off, -1, 3)
                if has(it, off, 0):
                    row_scores(it, off, 1)
                if has(it, off, 1):
                    pe.wait_ge(xtl_ready, i + 2)
                    product3(M0[:, 0:LQ], WQK_HI[:, 0:D], WQK_LO[:, 0:D], XT_HI[1 - u][:], XT_LO[1 - u][:]).then_inc(q_full, 1)
                if has(it, off, 0):
                    row_scores(it, off, 2)
                if has(it, off, -2):
                    pe.wait_ge(rn_ready, i - 1)
                    pe.wait_ge(x1_ready, i - 1)
                    for t in range(2):
                        mm = nc.tensor.transpose(M1[:, t * P:(t + 1) * P], RN[u][:, t, :], IDENT)
                    mm.then_inc(tx2_full, 1)
                if has(it, off, -1):
                    pe.wait_ge(p_ready, 4 * i)
                    wait(pe, at_ready, i - 1)
                    values(it, off, 1).then_inc(den_full, 1)
                if has(it, off, 0):
                    row_scores(it, off, 3)
                if has(it, off, -2):
                    pe.wait_ge(x2t_ready, i - 1)
                    for t in range(2):
                        mm = nc.tensor.matmul(M1[:, t * E:(t + 1) * E], X2T[u][:, t * P:(t + 1) * P], GATE[:], start=True, stop=True)
                    mm.then_inc(lg_full, 1)
                if has(it, off, 1):
                    select(it, off, 0)
                if has(it, off, -1):
                    pe.wait_ge(v2_ready, i)
                    values(it, off, 0).then_inc(pv_full, 1)
                if has(it, off, 0):
                    pe.wait_ge(m_ready, 4 * i + 4)
                    for t in range(2):
                        mm = nc.tensor.transpose(M0[0:1 + HEADS, t * P:(t + 1) * P], MNEG[u][:, t, :], IDENT)
                    mm.then_inc(mt_full, 1)
                if has(it, off, 1):
                    select(it, off, 1)
                if has(it, off, -1):
                    pe.wait_ge(at_ready, i)
                    if has(it, off, -2):
                        pe.wait_ge(logit_ready, i - 1)
                    for t in range(2):
                        mm = nc.tensor.matmul(M1[:, t * D:(t + 1) * D], AT[:, t * P:(t + 1) * P], WO[:], start=True, stop=True)
                    mm.then_inc(wo_full, 1)
                if has(it, off, 0):
                    scores(it, off, 0, 0)
                    scores(it, off, 0, 1)

            over_batches(pe, step)

            def turn_slots(tn, loads, v):
                pe.wait_ge(xl_in[v], 16 * loads)
                for c, (t0, nt) in enumerate(CHUNKS):
                    wait(pe, ex_ready, tn + (c - 1))
                    for t in range(nt):
                        mm = nc.tensor.transpose(TB[(3 * v + c) % 2][:, t * P:(t + 1) * P], XL[v][:, t0 + t, 0:D], IDENT)
                    mm.then_inc(tb_full, 1)

            def down(it, n, v, nt):
                pe.wait_ge(h_ready, 24 * it + 4 * (n + 1))
                if n >= 2 or not isinstance(it, int):
                    wait(pe, y_ready, 6 * it + (n - 1))
                for t in range(nt):
                    for f in range(FT):
                        mm = nc.tensor.matmul(Y_PS[n % 2][:, t * D:(t + 1) * D], H[n % 2][:, f, t * P:(t + 1) * P],
                                              W_RAW[v][:, 2 * F + f * D:2 * F + (f + 1) * D], start=(f == 0), stop=(f == FT - 1))
                mm.then_inc(dn_full, 1)

            turn_slots(0, 1, 0)

            def pair(it, last):
                for v in range(2):
                    pe.wait_ge(w_ready, 2 * it + (v + 1))
                    for c, (t0, nt) in enumerate(CHUNKS):
                        n = 3 * v + c
                        pe.wait_ge(ex_ready, 6 * it + (n + 1))
                        cols = slice(t0 * P, (t0 + nt) * P)
                        for f in range(FT):
                            m = 4 * n + f
                            for ps, w0, read, full in ((GATE_PS, 0, sg_ready, g_full), (UP_PS, F, h_ready, u_full)):
                                wait(pe, read, 24 * it + (m - 1))
                                w = slice(w0 + f * P, w0 + (f + 1) * P)
                                mm = product3(ps[m % 2][:, 0:nt * P], W_HI[v][:, w], W_LO[v][:, w], EX_HI[v][:, cols], EX_LO[v][:, cols])
                                mm.then_inc(full, 1)
                            if f == 1 and c > 0:
                                down(it, n - 1, v, CHUNKS[c - 1][1])
                    if not (last and v == 1):
                        turn_slots(6 * it + (3 * v + 3), it + (v + 1), 1 - v)
                    down(it, 3 * v + 2, v, CHUNKS[2][1])

            over_experts(pe, pair)

        @block.vector
        def _(dve):
            dve.wait_ge(mask_in, 16)
            nc.vector.tensor_copy(MASKF[:], MASKI[:]).then_inc(setup, 1)
            dve.wait_ge(setup, 1)
            nc.vector.tensor_reduce(ANY[:], MASKF[:], AX.X, ALU.max).then_inc(setup, 1)
            dve.wait_ge(setup, 2)
            dve.wait_ge(ctx_in, 16)
            any_b = ANY[:].unsqueeze(2).to_broadcast([P, B, LK])
            nc.vector.tensor_tensor(CTXM[:], CTX[:, :, 0, :], any_b, ALU.mult).then_inc(setup, 1)
            nc.vector.tensor_scalar(MASKF[:], MASKF[:], -1.0, BIG, ALU.add, ALU.mult).then_inc(setup, 1)
            dve.wait_ge(setup, 4)
            nc.vector.tensor_tensor(MASKF[:], MASKF[:], any_b, ALU.mult).then_inc(setup, 1)
            dve.wait_ge(wsplit, 1)
            nc.vector.tensor_tensor(WQK_LO[:], WQK[:], WQK_HI[:].bitcast(F32), ALU.subtract).then_inc(wsplit, 1)
            dve.wait_ge(ctx_split, 1)
            nc.vector.tensor_tensor(CTX_LO[:], CTXM[:].rearrange("p b k -> p (b k)"), CTX_HI[:].bitcast(F32), ALU.subtract
                                    ).then_inc(ctx_split, 1)
            dve.wait_ge(const_in, 16)
            nc.vector.tensor_copy(TRI[:], C[:, C_TRI:C_TRI + P]).then_inc(setup, 1)
            nc.vector.memset(ONES[:], 1.0)
            nc.vector.memset(SEENF[:], 0.0)
            nc.vector.memset(RALL[:, :, D:ROW], 0.0).then_inc(setup, 1)
            dve.wait_ge(setup, 7)
            nc.vector.tensor_copy(RALL[:, :, D + 2], C[:, C_TOKEN:C_TOKEN + TILES])
            for v in range(2):
                nc.vector.memset(MNEG[v][:], 1.0)
                nc.vector.memset(QS[v][ONE_ROW:ONE_ROW + 1, :, :].bitcast(F32), 1.0)
            nc.vector.memset(SEEN[:], 0.0).then_inc(setup, 1)
            for n in range(8):
                g, half = n // 2, n % 2
                dve.wait_ge(k_hi, n + 1)
                lo = KC[64:96, 8 * half:8 * half + 8, g, :]
                nc.vector.tensor_tensor(lo, MX[n % 2][64:96, :].rearrange("p (b k) -> p b k", k=LK), lo, ALU.subtract).then_inc(k_used, 1)
            dve.wait_ge(x_in, 64)
            for t in range(TILES):
                ins = nc.vector.bn_stats(STATS[:, t, :], X[:, t, :])
            ins.then_inc(setup, 1)
            dve.wait_ge(setup, 9)
            for t in range(TILES):
                ins = nc.vector.bn_aggr(MV[:, t, :], STATS[:, t, :])
            ins.then_inc(setup, 1)
            dve.wait_ge(setup, 10)
            nc.vector.tensor_scalar(VE[:], MV[:, :, 1], EPS, None, ALU.add).then_inc(ve_ready, 1)
            dve.wait_ge(rstd_ready, 1)

            def norm(i, v):
                wait(dve, tx_full, i - 1)
                for t in range(2):
                    tile = 2 * i + t
                    ins = nc.vector.tensor_scalar(
                        XN[v][:, t, :], X[:, bass.ds(tile, 1), :].rearrange("p a d -> p (a d)"),
                        MV[:, bass.ds(tile, 1), 0], RSTD[:, bass.ds(tile, 1)], ALU.subtract, ALU.mult)
                ins.then_inc(xn_ready, 1)

            norm(0, 0)

            ROUTE = 20

            def row_max(it, off, m):
                i, u = 2 * it + off, off % 2
                t, b = m // 2, m % 2
                dve.wait_ge(mx_full, 4 * i + (m + 1))
                if m == 0:
                    wait(dve, mt_full, i - 1)
                nc.vector.tensor_reduce(MNEG[u][:, t, 1 + 8 * b:9 + 8 * b], MX[b][:].rearrange("p (h k) -> p h k", k=LK),
                                        AX.X, ALU.max, negate=True).then_inc(m_ready, 1)

            def link(r, step):
                dve.wait_ge(route_step, ROUTE * r + step)

            def best(k, part, r, last):
                src = LOGIT if k == 0 else LOGIT2
                rev = C[:, C_REV:C_BASE].unsqueeze(1).to_broadcast([P, 4, E])
                top, code = TOP[:, k, :], CODE[:, k, :]
                if part == 0:
                    nc.vector.tensor_reduce(top, src[:], AX.X, ALU.max).then_inc(route_step, 1)
                elif part == 1:
                    link(r, last)
                    nc.vector.tensor_tensor(R1[:], src[:], top.unsqueeze(2).to_broadcast([P, 4, E]), ALU.is_equal).then_inc(route_step, 1)
                elif part == 2:
                    link(r, last)
                    nc.vector.tensor_tensor(R1[:], R1[:], rev, ALU.mult).then_inc(route_step, 1)
                elif part == 3:
                    link(r, last)
                    nc.vector.tensor_reduce(code, R1[:], AX.X, ALU.max).then_inc(route_step, 1)
                else:
                    link(r, last)
                    nc.vector.tensor_tensor(OH[:, :, k, :], rev, code.unsqueeze(2).to_broadcast([P, 4, E]), ALU.is_equal
                                            ).then_inc(route_step if k == 0 else oh_ready, 1)

            def choose(r, part):
                if part == 0:
                    dve.wait_ge(logit_ready, 2 * r + 2)
                if part < 5:
                    best(0, part, r, part)
                elif part == 5:
                    link(r, 5)
                    nc.vector.scalar_tensor_tensor(out=LOGIT2[:], in0=OH[:, :, 0, :], scalar=-3e38, in1=LOGIT[:], op0=ALU.mult, op1=ALU.add
                                                   ).then_inc(route_step, 1)
                elif part < 11:
                    if part == 6:
                        link(r, 6)
                    best(1, part - 6, r, part)
                if part == 10:
                    nc.vector.tensor_tensor(DELTA[:], TOP[:, 1, :], TOP[:, 0, :], ALU.subtract).then_inc(delta_ready, 1)

            def place(r, part):
                oh = OH[:].rearrange("p t k e -> p t (k e)")
                base = C[:, C_BASE:C_TRASH].unsqueeze(1).to_broadcast([P, 4, TOPK * E])
                spare = C[:, bass.ds(8 * r + C_TRASH, 4 * TOPK)].rearrange("p (t k) -> p t k", k=TOPK)
                first = RALL[:, bass.ds(4 * r, 4), D]
                second = RALL[:, bass.ds(4 * r, 4), D + 1]
                if part == 0:
                    dve.wait_ge(expd_ready, r + 1)
                    nc.vector.tensor_scalar(DEN[:], EXPD[:], 1.0, None, ALU.add).then_inc(route_step, 1)
                    dve.wait_ge(oh_ready, r + 1)
                    nc.vector.tensor_tensor(R2[:], oh, base, ALU.mult).then_inc(route_step, 1)
                elif part == 1:
                    link(r, 12)
                    nc.vector.reciprocal(first, DEN[:]).then_inc(route_step, 1)
                    nc.vector.tensor_reduce(SB[:], R2[:].rearrange("p t (k e) -> p t k e", k=TOPK), AX.X, ALU.add).then_inc(route_step, 1)
                elif part == 2:
                    link(r, 13)
                    nc.vector.tensor_tensor(second, EXPD[:], first, ALU.mult)
                    nc.vector.tensor_reduce(ADDED[:], OH[:].rearrange("p t k e -> p (k e) t"), AX.X, ALU.add).then_inc(route_step, 1)
                elif part == 3:
                    link(r, 15)
                    nc.vector.tensor_tensor(SEENF[:], SEENF[:], ADDED[:], ALU.add).then_inc(route_step, 1)
                elif part == 4:
                    dve.wait_ge(rk_full, r + 1)
                    nc.vector.tensor_tensor(R3[:], QP[:, 0:4 * TOPK * E].rearrange("p (t n) -> p t n", t=4), oh, ALU.mult).then_inc(rk_used, 1)
                elif part == 5:
                    dve.wait_ge(rk_used, r + 1)
                    nc.vector.tensor_reduce(RK[:], R3[:].rearrange("p t (k e) -> p t k e", k=TOPK), AX.X, ALU.add).then_inc(route_step, 1)
                    link(r, 16)
                    nc.vector.tensor_copy(SEEN[:], SEENF[:])
                elif part == 6:
                    link(r, 17)
                    nc.vector.tensor_scalar(OKAY[:], RK[:], float(CAP), None, ALU.is_lt)
                    nc.vector.tensor_tensor(SLOTF[:], SB[:], RK[:], ALU.add).then_inc(route_step, 1)
                elif part == 7:
                    link(r, 18)
                    nc.vector.tensor_tensor(SLOTF[:], SLOTF[:], spare, ALU.subtract).then_inc(route_step, 1)
                elif part == 8:
                    link(r, 19)
                    nc.vector.tensor_tensor(SLOTF[:], SLOTF[:], OKAY[:], ALU.mult).then_inc(route_step, 1)

            def routing(it, off, part):
                if off % 2 == 0 and has(it, off, -4):
                    choose(it + (off - 4) // 2, part)
                elif off % 2 == 1 and has(it, off, -5):
                    place(it + (off - 5) // 2, part)

            def step(it, off):
                i, u = 2 * it + off, off % 2
                if has(it, off, 0):
                    row_max(it, off, 0)
                routing(it, off, 0)
                if has(it, off, -2):
                    there = held(dve, 2 * i - 3)
                    dve.wait_ge(x_in, 64)
                    dve.wait_ge(ln2_step, there)
                    for t in range(2):
                        ins = nc.vector.bn_aggr(MV2[u][:, t, :], STATS2[u][:, t, :])
                    ins.then_inc(ln2_step, 1)
                if has(it, off, 1):
                    dve.wait_ge(xth_ready, i + 2)
                    nc.vector.tensor_tensor(XT_LO[1 - u][:], M0[:, 0:LQ], XT_HI[1 - u][:].bitcast(F32), ALU.subtract).then_inc(xtl_ready, 1)
                if has(it, off, -2):
                    dve.wait_ge(ln2_step, 2 * i - 2)
                    nc.vector.tensor_scalar(VE2[u][:], MV2[u][:, :, 1], EPS, None, ALU.add).then_inc(ve2_ready, 1)
                routing(it, off, 1)
                if has(it, off, 0):
                    row_max(it, off, 1)
                routing(it, off, 2)
                if has(it, off, 1):
                    dve.wait_ge(qhi_ready, i + 2)
                    wait(dve, sel_full, 2 * i + 2)
                    nc.vector.scalar_tensor_tensor(out=Q_LO[:], in0=M0[:, 0:LQ], scalar=SCALE, in1=Q_HI[:].bitcast(F32),
                                                   op0=ALU.mult, op1=ALU.subtract).then_inc(qlo_ready, 1)
                routing(it, off, 3)
                if has(it, off, -2):
                    dve.wait_ge(rstd2_ready, i - 1)
                    wait(dve, rows_kept, i - 3)
                    for t in range(2):
                        ins = nc.vector.tensor_scalar(
                            RN[u][:, t, :], X[:, bass.ds(2 * i + (t - 4), 1), :].rearrange("p a d -> p (a d)"),
                            MV2[u][:, t, 0:1], RSTD2[u][:, t:t + 1], ALU.subtract, ALU.mult)
                    ins.then_inc(rn_ready, 1)
                if has(it, off, 0):
                    row_max(it, off, 2)
                routing(it, off, 4)
                if has(it, off, 2):
                    norm(2 * it + (off + 2), u)
                routing(it, off, 5)
                if has(it, off, 0):
                    row_max(it, off, 3)
                routing(it, off, 6)
                if has(it, off, -2):
                    dve.wait_ge(lg_full, i - 1)
                    if u == 0 and has(it, off, -4):
                        link(it + (off - 4) // 2, 6)
                    nc.vector.tensor_copy(LOGIT[:, 2 * u:2 * u + 2, :], M1[:, 0:2 * E].rearrange("p (t e) -> p t e", e=E)
                                          ).then_inc(logit_ready, 1)
                if has(it, off, -1):
                    dve.wait_ge(guess_ready, i)
                    nc.vector.tensor_tensor(ERR[:], DEN_PS[:, 0:LQ], GUESS[:], ALU.mult).then_inc(newton_step, 1)
                routing(it, off, 7)
                if has(it, off, -1):
                    dve.wait_ge(newton_step, 2 * i - 1)
                    nc.vector.scalar_tensor_tensor(out=RNEG[:], in0=ERR[:], scalar=-2.0, in1=GUESS[:], op0=ALU.add, op1=ALU.mult
                                                   ).then_inc(newton_step, 1)
                routing(it, off, 8)
                if has(it, off, -1):
                    dve.wait_ge(pv_full, i)
                    dve.wait_ge(newton_step, 2 * i)
                    nc.vector.scalar_tensor_tensor(out=AT[:], in0=OUT_PS[:, 0:LQ], scalar=-1.0, in1=RNEG[:], op0=ALU.mult, op1=ALU.mult
                                                   ).then_inc(at_ready, 1)
                routing(it, off, 9)
                routing(it, off, 10)
                if has(it, off, -5):
                    r = it + (off - 5) // 2
                    link(r, ROUTE)
                    wait(dve, sent[1 - u], 64 * r)
                    t = 1 - u
                    spare = C[:, bass.ds(8 * r + (C_TRASH + 4 * t), 2 * TOPK)].rearrange("p (t k) -> p t k", k=TOPK)
                    nc.vector.tensor_tensor(SLOT[t][:].rearrange("p (t k) -> p t k", k=TOPK), SLOTF[:, 2 * t:2 * t + 2, :], spare,
                                            ALU.add).then_inc(slot_ready, 1)
                if has(it, off, -1):
                    dve.wait_ge(wo_full, i)
                    xv = X[:, bass.ds(2 * i - 2, 2), :]
                    nc.vector.tensor_tensor(xv, M1[:, 0:2 * D].rearrange("p (t d) -> p t d", t=2), xv, ALU.add).then_inc(x1_ready, 1)
                    there = held(dve, i)
                    dve.wait_ge(x_in, 64)
                    dve.wait_ge(x1_ready, there)
                    for t in range(2):
                        ins = nc.vector.bn_stats(STATS2[1 - u][:, t, :], X[:, bass.ds(2 * i + (t - 2), 1), :].rearrange("p a d -> p (a d)"))
                    ins.then_inc(ln2_step, 1)

            over_batches(dve, step)

            def slots_lo(tn, v):
                for c, (t0, nt) in enumerate(CHUNKS):
                    cols = slice(t0 * P, (t0 + nt) * P)
                    dve.wait_ge(ex_hi_ready, tn + (c + 1))
                    nc.vector.tensor_tensor(EX_LO[v][:, cols], TB[(3 * v + c) % 2][:, 0:nt * P], EX_HI[v][:, cols].bitcast(F32),
                                            ALU.subtract).then_inc(ex_ready, 1)

            def tokens_of(v, loads):
                dve.wait_ge(xl_in[v], 16 * loads)
                nc.vector.tensor_copy(IDX[v][:], XL[v][:, :, D + 2]).then_inc(idx_ready, 1)

            def weigh(it, n, v):
                t0, nt = CHUNKS[n % 3]
                dve.wait_ge(dn_full, 6 * it + (n + 1))
                wait(dve, returned[n % 2], 160 * it + 16 * RETURNS[n][n % 2])
                for t in range(nt):
                    k = (t0 + t) * P // CAP
                    ins = nc.vector.tensor_scalar(YS[n % 2][:, t, :], Y_PS[n % 2][:, t * D:(t + 1) * D],
                                                  XL[v][:, t0 + t, D + k:D + k + 1], None, ALU.mult)
                ins.then_inc(y_ready, 1)

            slots_lo(0, 0)
            tokens_of(0, 1)

            def pair(it, last):
                for v in range(2):
                    for c, (t0, nt) in enumerate(CHUNKS):
                        n = 3 * v + c
                        for f in range(FT):
                            m = 4 * n + f
                            dve.wait_ge(sg_ready, 24 * it + (m + 1))
                            dve.wait_ge(u_full, 24 * it + (m + 1))
                            if f == 0:
                                wait(dve, dn_full, 6 * it + (n - 1))
                            nc.vector.tensor_tensor(H[n % 2][:, f, 0:nt * P], SG[m % 2][:, 0:nt * P], UP_PS[m % 2][:, 0:nt * P],
                                                    ALU.mult).then_inc(h_ready, 1)
                            if f == 2 and c > 0:
                                weigh(it, n - 1, v)
                    if not (last and v == 1):
                        slots_lo(6 * it + (3 * v + 3), 1 - v)
                    weigh(it, 3 * v + 2, v)
                    if not (last and v == 1):
                        for w in range(2):
                            wait(dve, returned[w], 160 * it + 16 * RETURNS[3 * v][w])
                        tokens_of(1 - v, it + (v + 1))

            over_experts(dve, pair)
            for q in range(4):
                dve.wait_ge(fb_in[q], 32)
                xv = X[:, 8 * q:8 * q + 8, :]
                nc.vector.tensor_tensor(FB[0][q][:], FB[0][q][:], FB[1][q][:], ALU.add).then_inc(add_step, 1)
                dve.wait_ge(add_step, q + 1)
                nc.vector.tensor_tensor(xv, xv, FB[0][q][:], ALU.add).then_inc(out_ready, 1)


def kernel(**inputs):
    import concourse.bacc as bacc
    from concourse.bass_utils import run_bass_kernel_spmd

    a = {k: np.asarray(v) for k, v in inputs.items()}
    const, empty, zeros = constants()

    def stacked(w):
        g = w.reshape(D, GROUPS, 1, 32)
        return np.ascontiguousarray(np.broadcast_to(g, (D, GROUPS, 3, 32)).reshape(D, GROUPS * 96))

    ctx = a["ctx_1024"].transpose(2, 0, 1)[:, :, None, :]
    wg, wu, wd = (a["L0_ffn_" + n] for n in ("wi_gate", "wi_up", "wo"))
    arrays = {
        "x": np.ascontiguousarray(a["x"].reshape(TOKENS, D)),
        "ctx": np.ascontiguousarray(np.broadcast_to(ctx, (D, B, 2, LK))),
        "mask": np.ascontiguousarray(a["mask_BxS2_ik0"]),
        "wq": a["L0_xattn_Wq"],
        "wk": stacked(a["L0_xattn_Wk"]),
        "wv": a["L0_xattn_Wv"],
        "wo": a["L0_xattn_Wo"],
        "gate": np.ascontiguousarray(a["L0_ffn_gate_w"].T),
        "wgu": np.ascontiguousarray(np.concatenate([wg.transpose(0, 2, 1), wu.transpose(0, 2, 1)], axis=2)),
        "wdn": np.ascontiguousarray(wd.transpose(0, 2, 1).reshape(E, FT, P, D).transpose(0, 2, 1, 3).reshape(E, P, FT * D)),
        "const": const,
        "empty": empty,
        "zeros": zeros,
    }
    nc = bacc.Bacc("TRN2", target_bir_lowering=False, num_devices=1)
    args = [nc.dram_tensor(f"in_{n}", v.shape, mybir.dt.from_np(v.dtype), kind="ExternalInput").ap() for n, v in arrays.items()]
    args.append(nc.dram_tensor("out", (TOKENS, D), F32, kind="ExternalOutput").ap())
    program(nc, *args)
    r = run_bass_kernel_spmd(nc, [{f"in_{n}": v for n, v in arrays.items()}], core_ids=[0])
    return r.results[0]["out"].reshape(B, LQ, D)
```

```python
from contextlib import ExitStack

import concourse.bass as bass
import numpy as np
from concourse import mybir

F32 = mybir.dt.float32
F32R = mybir.dt.float32r
BF16 = mybir.dt.bfloat16
I32 = mybir.dt.int32
ALU = mybir.AluOpType
ACT = mybir.ActivationFunctionType
AX = mybir.AxisListType

P = 128
B, LQ, LK, D = 16, 256, 64, 128
HEADS, DPH = 16, 8
GROUPS, HG = 4, 4
TOKENS = B * LQ
TILES = TOKENS // P
E, F, TOPK = 8, 512, 2
CAP = int(TOKENS / E * 1.25)
ESLOTS = TOPK * CAP
SLOTS = E * ESLOTS
STILES = ESLOTS // P
ROW = 132
PIECES = 8
PIECE = TILES // PIECES
EPS = 1e-5
BIG = float(2.0 ** 127)
SCALE = DPH ** -0.5
ONE_ROW = 96
NROW = ONE_ROW + 1 + HEADS
FT = F // P
CHUNKS = [(0, 4), (4, 3), (7, 3)]

C_IDENT = 0
C_KMASK = C_IDENT + P
C_VMASK = C_KMASK + GROUPS * HG
C_REV = C_VMASK + 2 * P
C_BASE = C_REV + E
C_TRASH = C_BASE + TOPK * E
C_TOKEN = C_TRASH + TILES * TOPK
C_TRI = C_TOKEN + TILES
NCONST = C_TRI + P


def constants():
    c = np.zeros((P, NCONST), np.float32)
    p = np.arange(P)
    c[:, C_IDENT:C_IDENT + P] = np.eye(P)
    km = np.zeros((P, GROUPS, HG), np.float32)
    for r in range(ONE_ROW):
        km[r, :, (r % 32) // DPH] = 1
    km[ONE_ROW] = 1
    for h in range(HEADS):
        km[ONE_ROW + 1 + h, h // HG, h % HG] = 1
    c[:, C_KMASK:C_VMASK] = km.reshape(P, -1)
    vm = np.zeros((P, 2, GROUPS, HG, DPH), np.float32)
    for s in range(2):
        for half in range(2):
            vm[64 * half:64 * half + 64, s, :, 2 * s + half, :] = 1
    c[:, C_VMASK:C_REV] = vm.reshape(P, -1)
    c[:, C_REV:C_BASE] = E - np.arange(E)
    c[:, C_BASE:C_TRASH] = (np.arange(E)[None, :] * ESLOTS + np.arange(TOPK)[:, None] * CAP).reshape(-1)
    token = np.arange(TILES)[None, :] * P + p[:, None]
    c[:, C_TRASH:C_TOKEN] = (SLOTS + token[:, :, None] + TOKENS * np.arange(TOPK)).reshape(P, -1)
    c[:, C_TOKEN:C_TRI] = token
    c[:, C_TRI:] = p[:, None] < p[None, :]
    empty = np.zeros((ESLOTS, ROW), np.float32)
    empty[:, 130] = TOKENS + np.arange(ESLOTS)
    return c, empty, np.zeros((1024, D), np.float32)


def program(nc, x, ctx, mask, wq, wk, wv, wo, gate, wgu, wdn, const, empty, zeros, out):
    slots = nc.dram_tensor("slots", [SLOTS + TOPK * TOKENS, ROW], F32, kind="Internal").ap()
    back = [nc.dram_tensor(f"back{k}", [TOKENS + ESLOTS, D], F32, kind="Internal").ap() for k in range(TOPK)]
    x_t = x.rearrange("(t p) d -> p t d", p=P)
    out_t = out.rearrange("(t p) d -> p t d", p=P)

    with ExitStack() as stack:
        def sb(name, shape, dt=F32, where=stack):
            return where.enter_context(nc.sbuf_tensor(name, shape, dt))

        def sem(name):
            return stack.enter_context(nc.semaphore(name))

        X = sb("X", [P, TILES, D])
        C = sb("C", [P, NCONST])
        W_RAW = [sb(f"w_raw{v}", [P, 2 * F + FT * D]) for v in range(2)]
        W_HI = [sb(f"w_hi{v}", [P, 2 * F], F32R) for v in range(2)]
        W_LO = [sb(f"w_lo{v}", [P, 2 * F], F32R) for v in range(2)]
        XL = [sb(f"xl{v}", [P, STILES, ROW]) for v in range(2)]
        IDX = [sb(f"idx{v}", [P, STILES], I32) for v in range(2)]
        part1 = ExitStack()

        def s1(name, shape, dt=F32):
            return sb(name, shape, dt, part1)

        TRI = s1("tri", [P, P], BF16)
        ONES = s1("ones", [P, P], BF16)
        CTX = s1("ctx", [P, B, LK])
        CTXM = s1("ctxm", [P, B, LK])
        CTX_HI = s1("ctx_hi", [P, B * LK], F32R)
        CTX_LO = s1("ctx_lo", [P, B * LK], F32R)
        MASKI = s1("maski", [P, B, LK], I32)
        MASKF = s1("maskf", [P, B, LK])
        ANY = s1("any", [P, B])
        NW = D + GROUPS * 96
        WQK = s1("wqk", [P, NW])
        WQK_HI = s1("wqk_hi", [P, NW], F32R)
        WQK_LO = s1("wqk_lo", [P, NW], F32R)
        SEL_HI = s1("sel_hi", [P, GROUPS, 3, 32], F32R)
        SEL_LO = s1("sel_lo", [P, GROUPS, 3, 32], F32R)
        WV = s1("wv", [P, D])
        WO = s1("wo", [P, D])
        GATE = s1("gate", [P, E])
        KC = s1("kc", [P, B, GROUPS, LK])
        VALL = s1("vall", [P, B, D])
        STATS = s1("stats", [P, TILES, 6])
        MV = s1("mv", [P, TILES, 2])
        VE = s1("ve", [P, TILES])
        RSTD = s1("rstd", [P, TILES])
        HALF = s1("half", [P, TILES])
        XN = [s1(f"xn{v}", [P, 2, D]) for v in range(2)]
        XT_HI = [s1(f"xt_hi{v}", [P, LQ], F32R) for v in range(2)]
        XT_LO = [s1(f"xt_lo{v}", [P, LQ], F32R) for v in range(2)]
        Q_HI = s1("q_hi", [P, LQ], F32R)
        Q_LO = s1("q_lo", [P, LQ], F32R)
        QS = [s1(f"qs{v}", [P, GROUPS, LQ], F32R) for v in range(2)]
        KS = [s1(f"ks{v}", [P, GROUPS, HG * LK], F32R) for v in range(2)]
        V2 = [s1(f"v2{v}", [P, 2, GROUPS, 32]) for v in range(2)]
        MNEG = [s1(f"mneg{v}", [P, 2, 1 + HEADS]) for v in range(2)]
        PROBS = [s1(f"probs{v}", [P, GROUPS, 2, LQ]) for v in range(2)]
        LOGD = s1("logd", [P, LQ])
        GUESS = s1("guess", [P, LQ])
        ERR = s1("err", [P, LQ])
        RNEG = s1("rneg", [P, LQ])
        AT = s1("at", [P, LQ])
        STATS2 = [s1(f"stats2{v}", [P, 2, 6]) for v in range(2)]
        MV2 = [s1(f"mv2{v}", [P, 2, 2]) for v in range(2)]
        VE2 = [s1(f"ve2{v}", [P, 2]) for v in range(2)]
        RSTD2 = [s1(f"rstd2{v}", [P, 2]) for v in range(2)]
        RALL = s1("rall", [P, TILES, ROW])
        RN = [s1(f"rn{v}", [P, 2, D]) for v in range(2)]
        X2T = [s1(f"x2t{v}", [P, LQ]) for v in range(2)]
        ROWS = [s1(f"rows{v}", [P, 2, ROW]) for v in range(2)]
        LOGIT = s1("logit", [P, 4, E])
        LOGIT2 = s1("logit2", [P, 4, E])
        R1 = s1("r1", [P, 4, E])
        R2 = s1("r2", [P, 4, TOPK * E])
        R3 = s1("r3", [P, 4, TOPK * E])
        TOP = s1("top", [P, TOPK, 4])
        CODE = s1("code", [P, TOPK, 4])
        OH = s1("oh", [P, 4, TOPK, E], BF16)
        SEEN = s1("seen", [P, TOPK * E], BF16)
        SEENF = s1("seenf", [P, TOPK * E])
        ADDED = s1("added", [P, TOPK * E])
        DELTA = s1("delta", [P, 4])
        EXPD = s1("expd", [P, 4])
        DEN = s1("den", [P, 4])
        WEIGHT = s1("weight", [P, TOPK, 4])
        RK = s1("rk", [P, 4, TOPK])
        SB = s1("sb", [P, 4, TOPK])
        OKAY = s1("okay", [P, 4, TOPK])
        SLOTF = s1("slotf", [P, 4, TOPK])
        SLOT = [s1(f"slot{v}", [P, 2 * TOPK], I32) for v in range(2)]
        part1.close()
        part2 = ExitStack()

        def s2(name, shape, dt=F32):
            return sb(name, shape, dt, part2)

        EX_HI = [s2(f"ex_hi{v}", [P, ESLOTS], F32R) for v in range(2)]
        EX_LO = [s2(f"ex_lo{v}", [P, ESLOTS], F32R) for v in range(2)]
        SG = [s2(f"sg{v}", [P, 512]) for v in range(2)]
        H = [s2(f"h{v}", [P, FT, 512]) for v in range(2)]
        YS = [s2(f"ys{v}", [P, 4, D]) for v in range(2)]
        FB = [[s2(f"fb{k}{q}", [P, PIECE, D]) for q in range(PIECES)] for k in range(TOPK)]
        part2.close()

        BANK = [stack.enter_context(nc.psum_tensor(f"bank{i}", [P, 512], F32)) for i in range(8)]
        MX, ST, QP, DEN_PS, M0, M1 = BANK[0:2], BANK[2:4], BANK[4], BANK[5], BANK[6], BANK[7]
        OUT_PS = ST[1]
        K_PS = [MX[0], MX[1], QP, DEN_PS]
        GATE_PS, UP_PS, TB, Y_PS = BANK[0:2], BANK[2:4], BANK[4:6], BANK[6:8]

        const_in, mask_in, ctx_in, w_in = sem("const_in"), sem("mask_in"), sem("ctx_in"), sem("w_in")
        x_in = [sem(f"x_in{q}") for q in range(4)]
        ext_in, wqk_in = sem("ext_in"), sem("wqk_in")
        filled = sem("filled")
        raw_in = [sem(f"raw_in{v}") for v in range(2)]
        setup = sem("setup")
        wsplit = sem("wsplit")
        ctx_split = sem("ctx_split")
        pool_setup = sem("pool_setup")
        k_full, k_hi, k_used = sem("k_full"), sem("k_hi"), sem("k_used")
        v_full, v_used = sem("v_full"), sem("v_used")
        ve_ready, rstd_ready = sem("ve_ready"), sem("rstd_ready")
        xn_ready, tx_full, xth_ready, xtl_ready = sem("xn_ready"), sem("tx_full"), sem("xth_ready"), sem("xtl_ready")
        q_full, qhi_ready, qlo_ready = sem("q_full"), sem("qhi_ready"), sem("qlo_ready")
        sel_full, qs_ready = sem("sel_full"), sem("qs_ready")
        ks_ready, v2_ready = sem("ks_ready"), sem("v2_ready")
        mx_full, m_ready, mt_full, aug_ready = sem("mx_full"), sem("m_ready"), sem("mt_full"), sem("aug_ready")
        st_full, p_ready, den_full, pv_full = sem("st_full"), sem("p_ready"), sem("den_full"), sem("pv_full")
        logd_ready, guess_ready, newton_step = sem("logd_ready"), sem("guess_ready"), sem("newton_step")
        at_ready, wo_full, x1_ready = sem("at_ready"), sem("wo_full"), sem("x1_ready")
        ln2_step, ve2_ready, rstd2_ready, rn_ready = sem("ln2_step"), sem("ve2_ready"), sem("rstd2_ready"), sem("rn_ready")
        tx2_full, x2t_ready, lg_full, logit_ready = sem("tx2_full"), sem("x2t_ready"), sem("lg_full"), sem("logit_ready")
        route_step = sem("route_step")
        oh_ready, rk_full, delta_ready, expd_ready = sem("oh_ready"), sem("rk_full"), sem("delta_ready"), sem("expd_ready")
        rk_used, slot_ready, rows_ready = sem("rk_used"), sem("slot_ready"), sem("rows_ready")
        rows_kept = sem("rows_kept")
        sent = [sem(f"sent{v}") for v in range(2)]
        xl_in = [sem(f"xl_in{v}") for v in range(2)]
        w_hi_ready, w_ready = sem("w_hi_ready"), sem("w_ready")
        tb_full, ex_hi_ready, ex_ready, idx_ready = sem("tb_full"), sem("ex_hi_ready"), sem("ex_ready"), sem("idx_ready")
        g_full, u_full = sem("g_full"), sem("u_full")
        sg_ready, h_ready, dn_full, y_ready = sem("sg_ready"), sem("h_ready"), sem("dn_full"), sem("y_ready")
        returned = [sem(f"returned{v}") for v in range(2)]
        fb_in = [[sem(f"fb_in{k}{q}") for q in range(PIECES)] for k in range(TOPK)]
        add_step, out_ready, stored = sem("add_step"), sem("out_ready"), sem("stored")

        IDENT = C[:, C_IDENT:C_IDENT + P]
        KMASK = C[:, C_KMASK:C_VMASK]
        VMASK = C[:, C_VMASK:C_REV].rearrange("p (s g c) -> p s g c", s=2, g=GROUPS)

        def over_batches(eng, step):
            for i in range(-1, 8):
                step(0, i)
            with eng.Fori(4, 7) as it:
                step(it, 0)
                step(it, 1)
            for i in range(14, B + 6):
                step(0, i)

        def has(it, off, ahead):
            return not isinstance(it, int) or 0 <= off + ahead < B

        def wait(eng, s, value):
            if not isinstance(value, int) or value > 0:
                eng.wait_ge(s, value)

        def held(eng, value):
            return value if isinstance(value, int) else eng.to_reg(value)

        def over_experts(eng, pair):
            pair(0, False)
            with eng.Fori(1, E // 2 - 1) as it:
                pair(it, False)
            pair(E // 2 - 1, True)

        RETURNS = [[sum(CHUNKS[m % 3][1] for m in range(n) if m % 2 == w) for w in range(2)] for n in range(7)]

        block = stack.enter_context(nc.Block())

        @block.sync
        def _(sp):
            sp.dma_start(MASKI[:].rearrange("p b k -> p (b k)"),
                         mask.rearrange("b k -> (b k)").rearrange("(a n) -> a n", a=1).to_broadcast([P, B * LK])
                         ).then_inc(mask_in, 16)
            sp.dma_start(CTX[:], ctx).then_inc(ctx_in, 16)
            sp.dma_start(WQK[:, 0:D], wq).then_inc(wqk_in, 16)
            sp.dma_start(WQK[:, D:], wk).then_inc(wqk_in, 16)
            sp.dma_start(X[:, 0:8, :], x_t[:, 0:8, :]).then_inc(x_in[0], 16)
            sp.dma_start(C[:], const).then_inc(const_in, 16)
            sp.dma_start(WV[:], wv).then_inc(w_in, 16)
            for q in range(1, 4):
                sp.dma_start(X[:, 8 * q:8 * q + 8, :], x_t[:, 8 * q:8 * q + 8, :]).then_inc(x_in[q], 16)
            sp.dma_start(WO[:], wo).then_inc(w_in, 16)
            sp.dma_start(GATE[:], gate).then_inc(w_in, 16)
            sp.wait_ge(setup, 5)
            sp.wait_ge(pool_setup, 1)
            for g in range(GROUPS):
                sp.dma_start(KC[ONE_ROW:ONE_ROW + 1, :, g, :], MASKF[ONE_ROW:ONE_ROW + 1]).then_inc(ext_in, 16)
            for e in range(E):
                sp.dma_start(slots[e * ESLOTS:(e + 1) * ESLOTS, :], empty).then_inc(filled, 16)
            for k in range(TOPK):
                for q in range(TOKENS // 1024):
                    sp.dma_start(back[k][q * 1024:(q + 1) * 1024, :], zeros).then_inc(filled, 16)
            for v in range(2):
                sp.dma_start(W_RAW[v][:, 0:2 * F], wgu[v]).then_inc(raw_in[v], 16)
                sp.dma_start(W_RAW[v][:, 2 * F:], wdn[v]).then_inc(raw_in[v], 16)
            for v in range(2):
                sp.wait_ge(sent[v], 64 * (B // 2))
            for v in range(2):
                sp.dma_start(XL[v][:], slots[v * ESLOTS:(v + 1) * ESLOTS, :].rearrange("(t p) c -> p t c", p=P)
                             ).then_inc(xl_in[v], 16)

            def pair(it, last):
                for v in range(2):
                    if last:
                        continue
                    sp.wait_ge(y_ready, 6 * it + 3 * v + 3)
                    e = 2 * it + (v + 2)
                    sp.dma_start(W_RAW[v][:, 0:2 * F], wgu[bass.ds(e, 1)].rearrange("a p f -> (a p) f")).then_inc(raw_in[v], 16)
                    sp.dma_start(W_RAW[v][:, 2 * F:], wdn[bass.ds(e, 1)].rearrange("a p f -> (a p) f")).then_inc(raw_in[v], 16)
                    sp.dma_start(XL[v][:], slots[bass.ds(e * ESLOTS, ESLOTS), :].rearrange("(t p) c -> p t c", p=P)
                                 ).then_inc(xl_in[v], 16)

            over_experts(sp, pair)
            for k in range(TOPK):
                for v in range(2):
                    left = 16 * 10 * (E // 2)
                    if k == 0 and v == 1:
                        left -= 16 * CHUNKS[2][1]
                    sp.wait_ge(returned[v], left)
                for q in range(PIECES):
                    sp.dma_start(FB[k][q][:], back[k][q * PIECE * P:(q + 1) * PIECE * P, :].rearrange("(t p) d -> p t d", p=P)
                                 ).then_inc(fb_in[k][q], 16)
            for q in range(PIECES):
                sp.wait_ge(out_ready, q + 1)
                tiles = slice(q * PIECE, (q + 1) * PIECE)
                sp.dma_start(out_t[:, tiles, :], X[:, tiles, :]).then_inc(stored, 16)
            sp.wait_ge(stored, 16 * PIECES)

        @block.gpsimd
        def _(pool):
            nc.gpsimd.memset(KC[ONE_ROW:, :, :, :], 1.0).then_inc(pool_setup, 1)
            for v in range(2):
                ins = nc.gpsimd.memset(QS[v][ONE_ROW:ONE_ROW + 1, :, :].bitcast(F32), 1.0)
            ins.then_inc(pool_setup, 1)
            pool.wait_ge(pool_setup, 2)
            nc.gpsimd.memset(HALF[:], -0.5)
            nc.gpsimd.memset(ONES[:], 1.0)
            nc.gpsimd.memset(SEENF[:], 0.0)
            nc.gpsimd.memset(SEEN[:], 0.0)
            for v in range(2):
                nc.gpsimd.memset(MNEG[v][:], 1.0)
            nc.gpsimd.memset(RALL[:, :, D:ROW], 0.0)
            nc.gpsimd.memset(SEL_HI[:, :, 1, :].bitcast(F32), 0.0)
            nc.gpsimd.memset(SEL_LO[:].bitcast(F32), 0.0).then_inc(pool_setup, 1)
            pool.wait_ge(pool_setup, 3)
            pool.wait_ge(const_in, 16)
            ident_g = IDENT.rearrange("p (g c) -> p g c", g=GROUPS)
            for part, sel in ((0, SEL_HI), (2, SEL_HI), (1, SEL_LO)):
                ins = nc.gpsimd.tensor_copy(sel[:, :, part, :], ident_g)
            ins.then_inc(pool_setup, 1)
            nc.gpsimd.tensor_copy(TRI[:], C[:, C_TRI:C_TRI + P])
            nc.gpsimd.tensor_copy(RALL[:, :, D + 2], C[:, C_TOKEN:C_TOKEN + TILES]).then_inc(pool_setup, 1)

            def inverse_deviation(part, tiles):
                pool.wait_ge(ve_ready, part)
                nc.gpsimd.tensor_tensor(RSTD[:, tiles], VE[:, tiles], HALF[:, tiles], ALU.pow).then_inc(rstd_ready, 1)

            inverse_deviation(1, slice(0, 8))
            pool.wait_ge(const_in, 16)
            pool.wait_ge(k_used, 8)
            pool.wait_ge(ext_in, 64)

            def spread_keys(it, off, c):
                i = 2 * it + (off + c)
                v = (off + c) % 2
                wait(pool, st_full, 4 * i - 4)
                nc.gpsimd.tensor_tensor(
                    KS[v][0:NROW].rearrange("p g (h k) -> p g h k", h=HG),
                    KC[0:NROW, bass.ds(i, 1)].rearrange("p a g k -> p (a g) k").unsqueeze(2).to_broadcast([NROW, GROUPS, HG, LK]),
                    KMASK[0:NROW].rearrange("p (g h) -> p g h", g=GROUPS).unsqueeze(3).to_broadcast([NROW, GROUPS, HG, LK]),
                    ALU.mult).then_inc(ks_ready, 1)

            def spread_values(it, off):
                i = 2 * it + off
                if isinstance(it, int) and off == 0:
                    pool.wait_ge(v_used, 4)
                wait(pool, pv_full, i - 1)
                nc.gpsimd.tensor_tensor(
                    V2[off % 2][:].rearrange("p s g c -> p s (g c)"),
                    VALL[:, bass.ds(i, 1), :].to_broadcast([P, 2, D]),
                    VMASK.rearrange("p s g c -> p s (g c)"), ALU.mult).then_inc(v2_ready, 1)

            def inverse_deviation2(it, off):
                i, u = 2 * it + off, off % 2
                wait(pool, ve2_ready, i - 1)
                nc.gpsimd.tensor_tensor(RSTD2[u][:], VE2[u][:], HALF[:, 0:2], ALU.pow).then_inc(rstd2_ready, 1)

            def send(it, off, t):
                u = off % 2
                for k in range(TOPK):
                    nc.gpsimd.indirect_dma_start(
                        out=slots[:, :], out_offset=bass.IndirectOffsetOnAxis(ap=SLOT[u][:, TOPK * t + k:TOPK * t + k + 1], axis=0),
                        in_=ROWS[u][:, t, :], in_offset=None).then_inc(sent[u], 16)

            def step(it, off):
                i, u = 2 * it + off, off % 2
                late = isinstance(it, int) and off > B
                if has(it, off, -2) and not late:
                    inverse_deviation2(it, off)
                if has(it, off, -6):
                    ready = held(pool, i - 5)
                    pool.wait_ge(filled, 16 * (E + TOPK * TOKENS // 1024))
                    pool.wait_ge(slot_ready, ready)
                    pool.wait_ge(rows_ready, ready)
                    send(it, off, 0)
                if has(it, off, -2) and late:
                    inverse_deviation2(it, off)
                if has(it, off, 1):
                    spread_keys(it, off, 1)
                if isinstance(it, int) and -1 <= off < 2:
                    q = off + 2
                    inverse_deviation(q + 1, slice(8 * q, 8 * q + 8))
                if has(it, off, 0):
                    spread_values(it, off)
                if has(it, off, -6):
                    send(it, off, 1)

            over_batches(pool, step)

            def split_weights(e, v, loads):
                loaded, used = held(pool, 32 * loads), held(pool, 12 * e - 12)
                pool.wait_ge(const_in, 16)
                pool.wait_ge(raw_in[v], loaded)
                wait(pool, u_full, used)
                nc.gpsimd.tensor_copy(W_HI[v][:], W_RAW[v][:, 0:2 * F]).then_inc(w_hi_ready, 1)
                pool.wait_ge(w_hi_ready, e + 1)
                nc.gpsimd.tensor_tensor(W_LO[v][:], W_RAW[v][:, 0:2 * F], W_HI[v][:].bitcast(F32), ALU.subtract
                                        ).then_inc(w_ready, 1)


            def pair(it, last):
                for v in range(2):
                    if not (last and v == 1) and not (isinstance(it, int) and it == 0 and v == 0):
                        split_weights(2 * it + (v + 1), 1 - v, it + (v + 1))
                    for c, (t0, nt) in enumerate(CHUNKS):
                        n = 3 * v + c
                        rows = held(pool, 6 * it + (n + 1))
                        pool.wait_ge(filled, 16 * (E + TOPK * TOKENS // 1024))
                        pool.wait_ge(y_ready, rows)
                        for t in range(nt):
                            j = t0 + t
                            nc.gpsimd.indirect_dma_start(
                                out=back[j * P // CAP][:, :],
                                out_offset=bass.IndirectOffsetOnAxis(ap=IDX[v][:, j:j + 1], axis=0),
                                in_=YS[n % 2][:, t, :], in_offset=None).then_inc(returned[n % 2], 16)

            over_experts(pool, pair)
            for v in range(2):
                pool.wait_ge(returned[v], 16 * 10 * (E // 2))

        @block.scalar
        def _(act):
            nc.scalar.preload_act_table_set("natural_log_exp_and_others")
            act.wait_ge(wqk_in, 32)
            nc.scalar.copy(WQK_HI[:], WQK[:]).then_inc(wsplit, 1)
            act.wait_ge(setup, 3)
            nc.scalar.copy(CTX_HI[:], CTXM[:].rearrange("p b k -> p (b k)")).then_inc(ctx_split, 1)
            for n in range(8):
                g, half = n // 2, n % 2
                act.wait_ge(k_full, n + 1)
                nc.scalar.copy(KC[0:96, 8 * half:8 * half + 8, g, :].bitcast(F32R),
                               K_PS[n % 4][0:96, :].rearrange("p (b k) -> p b k", k=LK)).then_inc(k_hi, 1)

            def exps(it, off, c, j):
                i = 2 * it + (off + c)
                act.wait_ge(st_full, 4 * i + (j + 1))
                if j == 0:
                    wait(act, pv_full, i - 1)
                nc.scalar.activation(PROBS[(off + c) % 2][:, j].rearrange("p s q -> p (s q)"), ST[j % 2][:], ACT.Exp
                                     ).then_inc(p_ready, 1)

            def keep_values(n):
                act.wait_ge(v_full, n + 1)
                nc.scalar.copy(VALL[:, 4 * n:4 * n + 4, :], ST[n % 2][:].rearrange("p (b d) -> p b d", d=D)).then_inc(v_used, 1)

            def stack_queries(it, off, h):
                i, u = 2 * it + off, off % 2
                act.wait_ge(sel_full, 2 * i + (3 + h))
                if h == 0:
                    wait(act, st_full, 4 * i)
                nc.scalar.copy(QS[1 - u][0:96, 2 * h:2 * h + 2, :].rearrange("p g q -> p (g q)"), QP[0:96, :]).then_inc(qs_ready, 1)

            def step(it, off):
                i, u = 2 * it + off, off % 2
                if isinstance(it, int) and off in (B + 4, B + 5):
                    act.wait_ge(raw_in[off - B - 4], 32)
                    nc.scalar.copy(W_HI[off - B - 4][:], W_RAW[off - B - 4][:, 0:2 * F]).then_inc(w_hi_ready, 1)
                if u == 1 and has(it, off, -5):
                    act.wait_ge(delta_ready, it + ((off - 5) // 2 + 1))
                    nc.scalar.activation(EXPD[:], DELTA[:], ACT.Exp).then_inc(expd_ready, 1)
                if has(it, off, 1):
                    act.wait_ge(tx_full, i + 2)
                    wait(act, q_full, i)
                    nc.scalar.copy(XT_HI[1 - u][:], M0[:, 0:LQ]).then_inc(xth_ready, 1)
                first = isinstance(it, int) and off == -1
                if first:
                    keep_values(0)
                    keep_values(1)
                if has(it, off, -1):
                    exps(it, off, -1, 2)
                if has(it, off, -6):
                    act.wait_ge(slot_ready, i - 5)
                    act.wait_ge(rows_kept, i - 5)
                    wait(act, sent[u], 64 * it + 64 * ((off - 6) // 2))
                    nc.scalar.copy(ROWS[u][:], RALL[:, bass.ds(2 * i - 12, 2), :]).then_inc(rows_ready, 1)
                if has(it, off, -1):
                    exps(it, off, -1, 3)
                if has(it, off, 1):
                    act.wait_ge(q_full, i + 2)
                    nc.scalar.mul(Q_HI[:], M0[:, 0:LQ], SCALE).then_inc(qhi_ready, 1)
                if first:
                    keep_values(2)
                    keep_values(3)
                if has(it, off, -1):
                    act.wait_ge(den_full, i)
                    nc.scalar.activation(LOGD[:], DEN_PS[:, 0:LQ], ACT.Ln).then_inc(logd_ready, 1)
                if has(it, off, -2):
                    act.wait_ge(tx2_full, i - 1)
                    nc.scalar.copy(X2T[u][:], M1[:, 0:LQ]).then_inc(x2t_ready, 1)
                if has(it, off, -1):
                    act.wait_ge(logd_ready, i)
                    nc.scalar.activation(GUESS[:], LOGD[:], ACT.Exp, scale=-1.0).then_inc(guess_ready, 1)
                if has(it, off, -2):
                    nc.scalar.copy(RALL[:, bass.ds(2 * i - 4, 2), 0:D], RN[u][:]).then_inc(rows_kept, 1)
                if has(it, off, 1):
                    stack_queries(it, off, 0)
                if has(it, off, 0):
                    act.wait_ge(mt_full, i + 1)
                    nc.scalar.copy(QS[u][ONE_ROW:NROW, :, :],
                                   M0[0:1 + HEADS, 0:LQ].unsqueeze(1).to_broadcast([1 + HEADS, GROUPS, LQ])).then_inc(aug_ready, 1)
                if has(it, off, 1):
                    stack_queries(it, off, 1)
                if has(it, off, 0):
                    exps(it, off, 0, 0)
                    exps(it, off, 0, 1)

            over_batches(act, step)
            nc.scalar.preload_act_table_set("silu_and_others")

            def slots_hi(tn, v):
                for c, (t0, nt) in enumerate(CHUNKS):
                    act.wait_ge(tb_full, tn + (c + 1))
                    nc.scalar.copy(EX_HI[v][:, t0 * P:(t0 + nt) * P], TB[(3 * v + c) % 2][:, 0:nt * P]).then_inc(ex_hi_ready, 1)

            slots_hi(0, 0)

            def pair(it, last):
                for v in range(2):
                    for c, (t0, nt) in enumerate(CHUNKS):
                        for f in range(FT):
                            m = 12 * v + 4 * c + f
                            act.wait_ge(g_full, 24 * it + (m + 1))
                            wait(act, h_ready, 24 * it + (m - 1))
                            nc.scalar.activation(SG[m % 2][:, 0:nt * P], GATE_PS[m % 2][:, 0:nt * P], ACT.Silu).then_inc(sg_ready, 1)
                    if not (last and v == 1):
                        slots_hi(6 * it + (3 * v + 3), 1 - v)

            over_experts(act, pair)

        @block.tensor
        def _(pe):
            def product3(ps, hi, lo, m_hi, m_lo):
                nc.tensor.matmul(ps, hi, m_hi, start=True, stop=False)
                nc.tensor.matmul(ps, lo, m_hi, start=False, stop=False)
                return nc.tensor.matmul(ps, hi, m_lo, start=False, stop=True)

            pe.wait_ge(wsplit, 2)
            pe.wait_ge(ctx_split, 2)
            for n in range(8):
                g, half = n // 2, n % 2
                if n >= 4:
                    pe.wait_ge(k_used, n - 3)
                cols = slice(512 * half, 512 * half + 512)
                product3(K_PS[n % 4][0:96, :], WQK_HI[:, D + 96 * g:D + 96 * g + 96], WQK_LO[:, D + 96 * g:D + 96 * g + 96], CTX_HI[:, cols], CTX_LO[:, cols]
                         ).then_inc(k_full, 1)
            pe.wait_ge(k_used, 8)
            pe.wait_ge(pool_setup, 5)

            def row_scores(it, off, m):
                i, u = 2 * it + off, off % 2
                t, b = m // 2, m % 2
                if m == 0:
                    pe.wait_ge(qs_ready, 2 * i + 2)
                    pe.wait_ge(ks_ready, i + 1)
                wait(pe, m_ready, 4 * i + (m - 1))
                for gg in range(2):
                    g = 2 * b + gg
                    mm = nc.tensor.matmul(MX[b][:, gg * HG * LK:(gg + 1) * HG * LK],
                                          QS[u][0:ONE_ROW + 1, g, t * P:(t + 1) * P], KS[u][0:ONE_ROW + 1, g, :],
                                          start=True, stop=True)
                mm.then_inc(mx_full, 1)

            def scores(it, off, c, j):
                i, u = 2 * it + (off + c), (off + c) % 2
                if j == 0:
                    pe.wait_ge(aug_ready, i + 1)
                wait(pe, p_ready, 4 * i + (j - 1))
                if isinstance(it, int) and i == 0 and j < 2:
                    pe.wait_ge(v_used, 4)
                for s in range(2):
                    mm = nc.tensor.matmul(ST[j % 2][:, s * LQ:(s + 1) * LQ], KS[u][0:NROW, j, s * P:(s + 1) * P],
                                          QS[u][0:NROW, j, :], start=True, stop=True)
                mm.then_inc(st_full, 1)

            def select(it, off, h):
                i = 2 * it + off
                if h == 0:
                    pe.wait_ge(qlo_ready, i + 2)
                wait(pe, qs_ready, 2 * i + (2 + h))
                if h == 0 and off % 2 == 1 and has(it, off, -5):
                    pe.wait_ge(rk_used, it + ((off - 5) // 2 + 1))
                for gg in range(2):
                    g = 2 * h + gg
                    ps = QP[0:96, gg * LQ:(gg + 1) * LQ]
                    nc.tensor.matmul(ps, SEL_HI[:, g].rearrange("p a c -> p (a c)"), Q_HI[:], start=True, stop=False)
                    mm = nc.tensor.matmul(ps, SEL_LO[:, g].rearrange("p a c -> p (a c)"), Q_LO[:], start=False, stop=True)
                mm.then_inc(sel_full, 1)

            def project_values(n):
                pe.wait_ge(w_in, 48)
                if n >= 2:
                    pe.wait_ge(v_used, n - 1)
                for b in range(4):
                    for copy in range(2):
                        mm = nc.tensor.matmul(ST[n % 2][copy * LK:(copy + 1) * LK, b * D:(b + 1) * D], CTX[:, 4 * n + b, :], WV[:],
                                              start=True, stop=True)
                mm.then_inc(v_full, 1)

            def values(it, off, what):
                v = (off + 1) % 2
                for s in range(2):
                    for g in range(GROUPS):
                        w = V2[v][:, s, g, :] if what == 0 else VMASK[:, s, g, :]
                        mm = nc.tensor.matmul((OUT_PS, DEN_PS)[what][32 * g:32 * g + 32, 0:LQ], w,
                                              PROBS[v][:, g, s, :], start=(s == 0), stop=(s == 1))
                return mm

            def step(it, off):
                i, u = 2 * it + off, off % 2
                if has(it, off, 1):
                    pe.wait_ge(xn_ready, i + 2)
                    wait(pe, qlo_ready, i + 1)
                    for t in range(2):
                        mm = nc.tensor.transpose(M0[:, t * P:(t + 1) * P], XN[1 - u][:, t, :], IDENT)
                    mm.then_inc(tx_full, 1)
                first = isinstance(it, int) and off == -1
                if first:
                    project_values(0)
                    project_values(1)
                if has(it, off, 0):
                    row_scores(it, off, 0)
                if has(it, off, -1):
                    scores(it, off, -1, 2)
                if u == 1 and has(it, off, -5):
                    r = it + (off - 5) // 2
                    pe.wait_ge(oh_ready, r + 1)
                    n = TOPK * E
                    ranks = QP[:, 0:4 * n]
                    oh = OH[:].rearrange("p t k e -> p t (k e)")
                    nc.tensor.matmul(ranks, TRI[:], oh.rearrange("p t n -> p (t n)"), start=True, stop=False, skip_group_check=True)
                    for t in range(3):
                        nc.tensor.matmul(ranks[:, (t + 1) * n:], ONES[:], oh[:, t:t + 1, :].to_broadcast([P, 3 - t, n]),
                                         start=False, stop=False, skip_group_check=True)
                    nc.tensor.matmul(ranks, ONES[:], SEEN[:].unsqueeze(1).to_broadcast([P, 4, n]),
                                     start=False, stop=True, skip_group_check=True).then_inc(rk_full, 1)
                if has(it, off, -1):
                    scores(it, off, -1, 3)
                if has(it, off, 0):
                    row_scores(it, off, 1)
                if has(it, off, 0):
                    row_scores(it, off, 2)
                if has(it, off, 1):
                    pe.wait_ge(xtl_ready, i + 2)
                    product3(M0[:, 0:LQ], WQK_HI[:, 0:D], WQK_LO[:, 0:D], XT_HI[1 - u][:], XT_LO[1 - u][:]).then_inc(q_full, 1)
                if first:
                    project_values(2)
                    project_values(3)
                if has(it, off, -1):
                    pe.wait_ge(p_ready, 4 * i)
                    wait(pe, at_ready, i - 1)
                    values(it, off, 1).then_inc(den_full, 1)
                if has(it, off, 0):
                    row_scores(it, off, 3)
                if has(it, off, -2):
                    pe.wait_ge(rn_ready, i - 1)
                    pe.wait_ge(x1_ready, i - 1)
                    for t in range(2):
                        mm = nc.tensor.transpose(M1[:, t * P:(t + 1) * P], RN[u][:, t, :], IDENT)
                    mm.then_inc(tx2_full, 1)
                if has(it, off, 1):
                    select(it, off, 0)
                if has(it, off, -1):
                    pe.wait_ge(v2_ready, i)
                    values(it, off, 0).then_inc(pv_full, 1)
                if has(it, off, 0):
                    pe.wait_ge(m_ready, 4 * i + 4)
                    for t in range(2):
                        mm = nc.tensor.transpose(M0[0:1 + HEADS, t * P:(t + 1) * P], MNEG[u][:, t, :], IDENT)
                    mm.then_inc(mt_full, 1)
                if has(it, off, -2):
                    pe.wait_ge(x2t_ready, i - 1)
                    for t in range(2):
                        mm = nc.tensor.matmul(M1[:, t * E:(t + 1) * E], X2T[u][:, t * P:(t + 1) * P], GATE[:], start=True, stop=True)
                    mm.then_inc(lg_full, 1)
                if has(it, off, 1):
                    select(it, off, 1)
                if has(it, off, -1):
                    pe.wait_ge(at_ready, i)
                    if has(it, off, -2):
                        pe.wait_ge(logit_ready, i - 1)
                    for t in range(2):
                        mm = nc.tensor.matmul(M1[:, t * D:(t + 1) * D], AT[:, t * P:(t + 1) * P], WO[:], start=True, stop=True)
                    mm.then_inc(wo_full, 1)
                if has(it, off, 0):
                    scores(it, off, 0, 0)
                    scores(it, off, 0, 1)

            over_batches(pe, step)

            def turn_slots(tn, loads, v, chunks):
                pe.wait_ge(xl_in[v], 16 * loads)
                for c in chunks:
                    t0, nt = CHUNKS[c]
                    wait(pe, ex_ready, tn + (c - 1))
                    for t in range(nt):
                        mm = nc.tensor.transpose(TB[(3 * v + c) % 2][:, t * P:(t + 1) * P], XL[v][:, t0 + t, 0:D], IDENT)
                    mm.then_inc(tb_full, 1)

            def down(it, n, v, nt):
                pe.wait_ge(h_ready, 24 * it + 4 * (n + 1))
                if n >= 2 or not isinstance(it, int):
                    wait(pe, y_ready, 6 * it + (n - 1))
                for t in range(nt):
                    for f in range(FT):
                        mm = nc.tensor.matmul(Y_PS[n % 2][:, t * D:(t + 1) * D], H[n % 2][:, f, t * P:(t + 1) * P],
                                              W_RAW[v][:, 2 * F + f * D:2 * F + (f + 1) * D], start=(f == 0), stop=(f == FT - 1))
                mm.then_inc(dn_full, 1)

            turn_slots(0, 1, 0, (0, 1, 2))

            def pair(it, last):
                for v in range(2):
                    pe.wait_ge(w_ready, 2 * it + (v + 1))
                    for c, (t0, nt) in enumerate(CHUNKS):
                        n = 3 * v + c
                        pe.wait_ge(ex_ready, 6 * it + (n + 1))
                        cols = slice(t0 * P, (t0 + nt) * P)
                        for f in range(FT):
                            m = 4 * n + f
                            for ps, w0, read, full in ((GATE_PS, 0, sg_ready, g_full), (UP_PS, F, h_ready, u_full)):
                                wait(pe, read, 24 * it + (m - 1))
                                w = slice(w0 + f * P, w0 + (f + 1) * P)
                                mm = product3(ps[m % 2][:, 0:nt * P], W_HI[v][:, w], W_LO[v][:, w], EX_HI[v][:, cols], EX_LO[v][:, cols])
                                mm.then_inc(full, 1)
                            if f == 1 and c > 0:
                                down(it, n - 1, v, CHUNKS[c - 1][1])
                    if not (last and v == 1):
                        turn_slots(6 * it + (3 * v + 3), it + (v + 1), 1 - v, (0, 1))
                    down(it, 3 * v + 2, v, CHUNKS[2][1])
                    if not (last and v == 1):
                        turn_slots(6 * it + (3 * v + 3), it + (v + 1), 1 - v, (2,))

            over_experts(pe, pair)

        @block.vector
        def _(dve):
            dve.wait_ge(mask_in, 16)
            nc.vector.tensor_copy(MASKF[:], MASKI[:]).then_inc(setup, 1)
            dve.wait_ge(setup, 1)
            nc.vector.tensor_reduce(ANY[:], MASKF[:], AX.X, ALU.max).then_inc(setup, 1)
            dve.wait_ge(setup, 2)
            dve.wait_ge(ctx_in, 16)
            any_b = ANY[:].unsqueeze(2).to_broadcast([P, B, LK])
            nc.vector.tensor_tensor(CTXM[:], CTX[:], any_b, ALU.mult).then_inc(setup, 1)
            dve.wait_ge(wsplit, 1)
            nc.vector.tensor_tensor(WQK_LO[:], WQK[:], WQK_HI[:].bitcast(F32), ALU.subtract).then_inc(wsplit, 1)
            dve.wait_ge(ctx_split, 1)
            nc.vector.tensor_tensor(CTX_LO[:], CTXM[:].rearrange("p b k -> p (b k)"), CTX_HI[:].bitcast(F32), ALU.subtract
                                    ).then_inc(ctx_split, 1)

            nc.vector.tensor_scalar(MASKF[:], MASKF[:], -1.0, BIG, ALU.add, ALU.mult).then_inc(setup, 1)
            dve.wait_ge(setup, 4)
            nc.vector.tensor_tensor(MASKF[:], MASKF[:], any_b, ALU.mult).then_inc(setup, 1)

            def statistics(first, last):
                for t in range(first, last):
                    if t % 8 == 0:
                        dve.wait_ge(x_in[t // 8], 16)
                    ins = nc.vector.bn_stats(STATS[:, t, :], X[:, t, :])
                return ins

            def mean_and_variance(first, last, steps):
                dve.wait_ge(setup, steps)
                for t in range(first, last):
                    ins = nc.vector.bn_aggr(MV[:, t, :], STATS[:, t, :])
                ins.then_inc(setup, 1)
                dve.wait_ge(setup, steps + 1)
                nc.vector.tensor_scalar(VE[:, first:last], MV[:, first:last, 1], EPS, None, ALU.add).then_inc(ve_ready, 1)

            statistics(0, 8).then_inc(setup, 1)
            mean_and_variance(0, 8, 6)
            for n in range(8):
                g, half = n // 2, n % 2
                dve.wait_ge(k_hi, n + 1)
                lo = KC[64:96, 8 * half:8 * half + 8, g, :]
                nc.vector.tensor_tensor(lo, K_PS[n % 4][64:96, :].rearrange("p (b k) -> p b k", k=LK), lo, ALU.subtract).then_inc(k_used, 1)
            dve.wait_ge(pool_setup, 5)

            def norm(i, v):
                dve.wait_ge(rstd_ready, i // 4 + 1 if isinstance(i, int) else 4)
                wait(dve, tx_full, i - 1)
                xv, mv, rstd = X[:, bass.ds(2 * i, 2), :], MV[:, bass.ds(2 * i, 2), :], RSTD[:, bass.ds(2 * i, 2)]
                for t in range(2):
                    ins = nc.vector.tensor_scalar(XN[v][:, t, :], xv[:, t, :], mv[:, t, 0:1], rstd[:, t:t + 1], ALU.subtract, ALU.mult)
                ins.then_inc(xn_ready, 1)

            norm(0, 0)

            ROUTE = 20

            def row_max(it, off, m):
                i, u = 2 * it + off, off % 2
                t, b = m // 2, m % 2
                dve.wait_ge(mx_full, 4 * i + (m + 1))
                if m == 0:
                    wait(dve, mt_full, i - 1)
                nc.vector.tensor_reduce(MNEG[u][:, t, 1 + 8 * b:9 + 8 * b], MX[b][:].rearrange("p (h k) -> p h k", k=LK),
                                        AX.X, ALU.max, negate=True).then_inc(m_ready, 1)

            def link(r, step):
                dve.wait_ge(route_step, ROUTE * r + step)

            def best(k, part, r, last):
                src = LOGIT if k == 0 else LOGIT2
                rev = C[:, C_REV:C_BASE].unsqueeze(1).to_broadcast([P, 4, E])
                top, code = TOP[:, k, :], CODE[:, k, :]
                if part == 0:
                    nc.vector.tensor_reduce(top, src[:], AX.X, ALU.max).then_inc(route_step, 1)
                elif part == 1:
                    link(r, last)
                    nc.vector.tensor_tensor(R1[:], src[:], top.unsqueeze(2).to_broadcast([P, 4, E]), ALU.is_equal).then_inc(route_step, 1)
                elif part == 2:
                    link(r, last)
                    nc.vector.tensor_tensor(R1[:], R1[:], rev, ALU.mult).then_inc(route_step, 1)
                elif part == 3:
                    link(r, last)
                    nc.vector.tensor_reduce(code, R1[:], AX.X, ALU.max).then_inc(route_step, 1)
                else:
                    link(r, last)
                    nc.vector.tensor_tensor(OH[:, :, k, :], rev, code.unsqueeze(2).to_broadcast([P, 4, E]), ALU.is_equal
                                            ).then_inc(route_step if k == 0 else oh_ready, 1)

            def choose(r, part):
                if part == 0:
                    dve.wait_ge(logit_ready, 2 * r + 2)
                if part < 5:
                    best(0, part, r, part)
                elif part == 5:
                    link(r, 5)
                    nc.vector.scalar_tensor_tensor(out=LOGIT2[:], in0=OH[:, :, 0, :], scalar=-3e38, in1=LOGIT[:], op0=ALU.mult, op1=ALU.add
                                                   ).then_inc(route_step, 1)
                elif part < 11:
                    if part == 6:
                        link(r, 6)
                    best(1, part - 6, r, part)
                if part == 10:
                    nc.vector.tensor_tensor(DELTA[:], TOP[:, 1, :], TOP[:, 0, :], ALU.subtract).then_inc(delta_ready, 1)

            def place(r, part):
                oh = OH[:].rearrange("p t k e -> p t (k e)")
                base = C[:, C_BASE:C_TRASH].unsqueeze(1).to_broadcast([P, 4, TOPK * E])
                if part == 0:
                    dve.wait_ge(expd_ready, r + 1)
                    nc.vector.tensor_scalar(DEN[:], EXPD[:], 1.0, None, ALU.add).then_inc(route_step, 1)
                    dve.wait_ge(oh_ready, r + 1)
                    nc.vector.tensor_tensor(R2[:], oh, base, ALU.mult).then_inc(route_step, 1)
                elif part == 1:
                    link(r, 12)
                    nc.vector.reciprocal(WEIGHT[:, 0, :], DEN[:]).then_inc(route_step, 1)
                    nc.vector.tensor_reduce(SB[:], R2[:].rearrange("p t (k e) -> p t k e", k=TOPK), AX.X, ALU.add).then_inc(route_step, 1)
                elif part == 3:
                    link(r, 13)
                    nc.vector.tensor_tensor(WEIGHT[:, 1, :], EXPD[:], WEIGHT[:, 0, :], ALU.mult)
                    nc.vector.tensor_reduce(ADDED[:], OH[:].rearrange("p t k e -> p (k e) t"), AX.X, ALU.add).then_inc(route_step, 1)
                elif part == 4:
                    link(r, 15)
                    nc.vector.tensor_tensor(SEENF[:], SEENF[:], ADDED[:], ALU.add).then_inc(route_step, 1)
                elif part == 2:
                    dve.wait_ge(rk_full, r + 1)
                    nc.vector.tensor_tensor(R3[:], QP[:, 0:4 * TOPK * E].rearrange("p (t n) -> p t n", t=4), oh, ALU.mult).then_inc(rk_used, 1)
                elif part == 5:
                    dve.wait_ge(rk_used, r + 1)
                    nc.vector.tensor_reduce(RK[:], R3[:].rearrange("p t (k e) -> p t k e", k=TOPK), AX.X, ALU.add).then_inc(route_step, 1)
                    link(r, 16)
                    nc.vector.tensor_copy(SEEN[:], SEENF[:])
                    nc.vector.tensor_copy(RALL[:, bass.ds(4 * r, 4), D:D + TOPK], WEIGHT[:].rearrange("p k t -> p t k"))
                elif part == 6:
                    link(r, 17)
                    nc.vector.tensor_scalar(OKAY[:], RK[:], float(CAP), None, ALU.is_lt)
                    nc.vector.tensor_tensor(SLOTF[:], SB[:], RK[:], ALU.add).then_inc(route_step, 1)
                elif part == 7:
                    link(r, 18)
                    spare = C[:, bass.ds(8 * r + C_TRASH, 4 * TOPK)].rearrange("p (t k) -> p t k", k=TOPK)
                    nc.vector.tensor_tensor(SLOTF[:], SLOTF[:], spare, ALU.subtract).then_inc(route_step, 1)
                elif part == 8:
                    link(r, 19)
                    nc.vector.tensor_tensor(SLOTF[:], SLOTF[:], OKAY[:], ALU.mult).then_inc(route_step, 1)

            def routing(it, off, part):
                if off % 2 == 0 and has(it, off, -4):
                    choose(it + (off - 4) // 2, part)
                elif off % 2 == 1 and has(it, off, -5):
                    place(it + (off - 5) // 2, part)

            def slots_of(it, off):
                i, u = 2 * it + off, off % 2
                r = it + (off - 5) // 2
                link(r, ROUTE)
                wait(dve, sent[1 - u], 64 * r)
                t = 1 - u
                spare = C[:, bass.ds(8 * r + (C_TRASH + 4 * t), 2 * TOPK)].rearrange("p (t k) -> p t k", k=TOPK)
                nc.vector.tensor_tensor(SLOT[t][:].rearrange("p (t k) -> p t k", k=TOPK), SLOTF[:, 2 * t:2 * t + 2, :], spare,
                                        ALU.add).then_inc(slot_ready, 1)

            def step(it, off):
                i, u = 2 * it + off, off % 2
                late = isinstance(it, int) and off > B
                if isinstance(it, int) and off in (B + 4, B + 5):
                    dve.wait_ge(w_hi_ready, off - B - 3)
                    nc.vector.tensor_tensor(W_LO[off - B - 4][:], W_RAW[off - B - 4][:, 0:2 * F], W_HI[off - B - 4][:].bitcast(F32), ALU.subtract
                                            ).then_inc(w_ready, 1)
                if has(it, off, 0):
                    row_max(it, off, 0)
                if has(it, off, -2):
                    there = held(dve, 2 * i - 3)
                    dve.wait_ge(x_in[3], 16)
                    dve.wait_ge(ln2_step, there)
                    for t in range(2):
                        ins = nc.vector.bn_aggr(MV2[u][:, t, :], STATS2[u][:, t, :])
                    ins.then_inc(ln2_step, 1)
                if has(it, off, 1):
                    dve.wait_ge(xth_ready, i + 2)
                    nc.vector.tensor_tensor(XT_LO[1 - u][:], M0[:, 0:LQ], XT_HI[1 - u][:].bitcast(F32), ALU.subtract).then_inc(xtl_ready, 1)
                routing(it, off, 0)
                if has(it, off, -2):
                    dve.wait_ge(ln2_step, 2 * i - 2)
                    nc.vector.tensor_scalar(VE2[u][:], MV2[u][:, :, 1], EPS, None, ALU.add).then_inc(ve2_ready, 1)
                for part in range(1, 11 if late else 2):
                    routing(it, off, part)
                if late and has(it, off, -5):
                    slots_of(it, off)
                if has(it, off, 0):
                    row_max(it, off, 1)
                if not late:
                    routing(it, off, 2)
                if has(it, off, 1):
                    dve.wait_ge(qhi_ready, i + 2)
                    wait(dve, sel_full, 2 * i + 2)
                    nc.vector.scalar_tensor_tensor(out=Q_LO[:], in0=M0[:, 0:LQ], scalar=SCALE, in1=Q_HI[:].bitcast(F32),
                                                   op0=ALU.mult, op1=ALU.subtract).then_inc(qlo_ready, 1)
                if not late:
                    routing(it, off, 3)
                if has(it, off, -2):
                    dve.wait_ge(rstd2_ready, i - 1)
                    wait(dve, rows_kept, i - 3)
                    xv = X[:, bass.ds(2 * i - 4, 2), :]
                    for t in range(2):
                        ins = nc.vector.tensor_scalar(
                            RN[u][:, t, :], xv[:, t, :],
                            MV2[u][:, t, 0:1], RSTD2[u][:, t:t + 1], ALU.subtract, ALU.mult)
                    ins.then_inc(rn_ready, 1)
                if has(it, off, 0):
                    row_max(it, off, 2)
                if not late:
                    routing(it, off, 4)
                if not late:
                    routing(it, off, 5)
                if has(it, off, 0):
                    row_max(it, off, 3)
                if not late:
                    routing(it, off, 6)
                if has(it, off, -1):
                    dve.wait_ge(guess_ready, i)
                    nc.vector.tensor_tensor(ERR[:], DEN_PS[:, 0:LQ], GUESS[:], ALU.mult).then_inc(newton_step, 1)
                if not late:
                    routing(it, off, 7)
                if has(it, off, -1):
                    dve.wait_ge(newton_step, 2 * i - 1)
                    nc.vector.scalar_tensor_tensor(out=RNEG[:], in0=ERR[:], scalar=-2.0, in1=GUESS[:], op0=ALU.add, op1=ALU.mult
                                                   ).then_inc(newton_step, 1)
                if not late:
                    routing(it, off, 8)
                if has(it, off, -1):
                    dve.wait_ge(pv_full, i)
                    dve.wait_ge(newton_step, 2 * i)
                    nc.vector.scalar_tensor_tensor(out=AT[:], in0=OUT_PS[:, 0:LQ], scalar=-1.0, in1=RNEG[:], op0=ALU.mult, op1=ALU.mult
                                                   ).then_inc(at_ready, 1)
                if has(it, off, -2):
                    dve.wait_ge(lg_full, i - 1)
                    if u == 0 and has(it, off, -4):
                        link(it + (off - 4) // 2, 6)
                    nc.vector.tensor_copy(LOGIT[:, 2 * u:2 * u + 2, :], M1[:, 0:2 * E].rearrange("p (t e) -> p t e", e=E)
                                          ).then_inc(logit_ready, 1)
                if has(it, off, 2):
                    norm(2 * it + (off + 2), u)
                if not late:
                    routing(it, off, 9)
                if not late:
                    routing(it, off, 10)
                if has(it, off, -1):
                    dve.wait_ge(wo_full, i)
                    xv = X[:, bass.ds(2 * i - 2, 2), :]
                    nc.vector.tensor_tensor(xv, M1[:, 0:2 * D].rearrange("p (t d) -> p t d", t=2), xv, ALU.add).then_inc(x1_ready, 1)
                if has(it, off, -5) and not late:
                    slots_of(it, off)
                if has(it, off, -1):
                    there = held(dve, i)
                    dve.wait_ge(x_in[3], 16)
                    dve.wait_ge(x1_ready, there)
                    for t in range(2):
                        ins = nc.vector.bn_stats(STATS2[1 - u][:, t, :], xv[:, t, :])
                    ins.then_inc(ln2_step, 1)
                if isinstance(it, int) and -1 <= off < 2:
                    q = off + 2
                    statistics(8 * q, 8 * q + 8).then_inc(setup, 1)
                    mean_and_variance(8 * q, 8 * q + 8, 2 * q + 6)

            over_batches(dve, step)

            def slots_lo(tn, v):
                for c, (t0, nt) in enumerate(CHUNKS):
                    cols = slice(t0 * P, (t0 + nt) * P)
                    dve.wait_ge(ex_hi_ready, tn + (c + 1))
                    nc.vector.tensor_tensor(EX_LO[v][:, cols], TB[(3 * v + c) % 2][:, 0:nt * P], EX_HI[v][:, cols].bitcast(F32),
                                            ALU.subtract).then_inc(ex_ready, 1)

            def tokens_of(v, loads):
                dve.wait_ge(xl_in[v], 16 * loads)
                nc.vector.tensor_copy(IDX[v][:], XL[v][:, :, D + 2]).then_inc(idx_ready, 1)

            def weigh(it, n, v):
                t0, nt = CHUNKS[n % 3]
                dve.wait_ge(dn_full, 6 * it + (n + 1))
                wait(dve, returned[n % 2], 160 * it + 16 * RETURNS[n][n % 2])
                for t in range(nt):
                    k = (t0 + t) * P // CAP
                    ins = nc.vector.tensor_scalar(YS[n % 2][:, t, :], Y_PS[n % 2][:, t * D:(t + 1) * D],
                                                  XL[v][:, t0 + t, D + k:D + k + 1], None, ALU.mult)
                ins.then_inc(y_ready, 1)

            slots_lo(0, 0)
            tokens_of(0, 1)

            def pair(it, last):
                for v in range(2):
                    for c, (t0, nt) in enumerate(CHUNKS):
                        n = 3 * v + c
                        for f in range(FT):
                            m = 4 * n + f
                            dve.wait_ge(sg_ready, 24 * it + (m + 1))
                            dve.wait_ge(u_full, 24 * it + (m + 1))
                            if f == 0:
                                wait(dve, dn_full, 6 * it + (n - 1))
                            nc.vector.tensor_tensor(H[n % 2][:, f, 0:nt * P], SG[m % 2][:, 0:nt * P], UP_PS[m % 2][:, 0:nt * P],
                                                    ALU.mult).then_inc(h_ready, 1)
                            if f == 2 and c > 0:
                                weigh(it, n - 1, v)
                    if not (last and v == 1):
                        slots_lo(6 * it + (3 * v + 3), 1 - v)
                    weigh(it, 3 * v + 2, v)
                    if not (last and v == 1):
                        for w in range(2):
                            wait(dve, returned[w], 160 * it + 16 * RETURNS[3 * v][w])
                        tokens_of(1 - v, it + (v + 1))

            over_experts(dve, pair)
            for q in range(PIECES):
                dve.wait_ge(fb_in[0][q], 16)
                xv = X[:, q * PIECE:(q + 1) * PIECE, :]
                nc.vector.tensor_tensor(xv, xv, FB[0][q][:], ALU.add).then_inc(add_step, 1)
            for q in range(PIECES):
                dve.wait_ge(fb_in[1][q], 16)
                dve.wait_ge(add_step, q + 1)
                xv = X[:, q * PIECE:(q + 1) * PIECE, :]
                nc.vector.tensor_tensor(xv, xv, FB[1][q][:], ALU.add).then_inc(out_ready, 1)


def kernel(**inputs):
    import concourse.bacc as bacc
    from concourse.bass_utils import run_bass_kernel_spmd

    a = {k: np.asarray(v) for k, v in inputs.items()}
    const, empty, zeros = constants()

    def stacked(w):
        g = w.reshape(D, GROUPS, 1, 32)
        return np.ascontiguousarray(np.broadcast_to(g, (D, GROUPS, 3, 32)).reshape(D, GROUPS * 96))

    wg, wu, wd = (a["L0_ffn_" + n] for n in ("wi_gate", "wi_up", "wo"))
    arrays = {
        "x": np.ascontiguousarray(a["x"].reshape(TOKENS, D)),
        "ctx": np.ascontiguousarray(a["ctx_1024"].transpose(2, 0, 1)),
        "mask": np.ascontiguousarray(a["mask_BxS2_ik0"]),
        "wq": a["L0_xattn_Wq"],
        "wk": stacked(a["L0_xattn_Wk"]),
        "wv": a["L0_xattn_Wv"],
        "wo": a["L0_xattn_Wo"],
        "gate": np.ascontiguousarray(a["L0_ffn_gate_w"].T),
        "wgu": np.ascontiguousarray(np.concatenate([wg.transpose(0, 2, 1), wu.transpose(0, 2, 1)], axis=2)),
        "wdn": np.ascontiguousarray(wd.transpose(0, 2, 1).reshape(E, FT, P, D).transpose(0, 2, 1, 3).reshape(E, P, FT * D)),
        "const": const,
        "empty": empty,
        "zeros": zeros,
    }
    nc = bacc.Bacc("TRN2", target_bir_lowering=False, num_devices=1)
    args = [nc.dram_tensor(f"in_{n}", v.shape, mybir.dt.from_np(v.dtype), kind="ExternalInput").ap() for n, v in arrays.items()]
    args.append(nc.dram_tensor("out", (TOKENS, D), F32, kind="ExternalOutput").ap())
    program(nc, *args)
    r = run_bass_kernel_spmd(nc, [{f"in_{n}": v for n, v in arrays.items()}], core_ids=[0])
    return r.results[0]["out"].reshape(B, LQ, D)
```
